# Optimizing a Trainium2 kernel written in Bass

```python
import numpy as np
import jax
import jax.numpy as jnp

def _softmax(x, axis=-1):
    return jax.nn.softmax(x, axis=axis)

def _gelu(x):
    return jax.nn.gelu(x, approximate=True)

def _silu(x):
    return jax.nn.silu(x)

def _sigmoid(x):
    return jax.nn.sigmoid(x)

def _layernorm(x, axis=-1, eps=1e-05):
    m = jnp.mean(x, axis=axis, keepdims=True)
    v = jnp.var(x, axis=axis, keepdims=True)
    return (x - m) / jnp.sqrt(v + eps)

def _scatter_add(tgt, idx, src, axis=0):
    return tgt.at[idx].add(src)

def _segment_sum(src, seg, n):
    return jax.ops.segment_sum(src, seg, n)
kernel_name = 'mk_gnn_resnorm_d1_gnn_r8_572336'

def setup_inputs(seed: int=0):
    np.random.seed(seed)
    _w = jnp.asarray

    def _rec_inputs():
        import jax
        import jax.numpy as jnp
        _gk = jax.random.key(seed)
        x = -0.0005121 + 1.001 * jax.random.normal(jax.random.fold_in(_gk, 1), (12500, 64), jnp.float32)
        src = jax.random.randint(jax.random.fold_in(_gk, 2), (200000,), 0, 12500, jnp.int32)
        dst = jnp.minimum((12500 * jax.random.uniform(jax.random.fold_in(_gk, 3), (200000,)) ** 2.0).astype(jnp.int32), 99999)
        _o = jnp.argsort(dst, stable=True)
        src = src[_o]
        dst = dst[_o]
        edge_attr_64 = -9.77346e-05 + 0.999888 * jax.random.normal(jax.random.fold_in(_gk, 11), (200000, 64), jnp.float32)
        return (x, src, dst, edge_attr_64)
    x, src, dst, edge_attr_64 = _rec_inputs()

    def _L0_gnn_setup():
        import jax, jax.numpy as jnp
        import numpy as np
        N_NODES = 6250
        N_EDGES = 100000
        EDGE_DIM = 64
        HID = 64
        key = jax.random.key(seed)
        ks = jax.random.split(key, 8)
        hidden_atom_emb = jax.random.normal(ks[0], (N_NODES, HID), dtype=jnp.float32)
        edge_emb = jax.random.normal(ks[1], (N_EDGES, EDGE_DIM), dtype=jnp.float32)
        edge_list = jax.random.randint(ks[2], (N_EDGES, 2), 0, N_NODES, dtype=jnp.int64)
        lim1 = float(np.sqrt(6.0 / (EDGE_DIM + HID)))
        W1 = jax.random.uniform(ks[3], (EDGE_DIM, HID), minval=-lim1, maxval=lim1, dtype=jnp.float32)
        b1 = jnp.zeros((HID,), dtype=jnp.float32)
        lim2 = float(np.sqrt(6.0 / (HID + HID)))
        W2 = jax.random.uniform(ks[4], (HID, HID), minval=-lim2, maxval=lim2, dtype=jnp.float32)
        b2 = jnp.zeros((HID,), dtype=jnp.float32)
        lim3 = 1.414 * float(np.sqrt(6.0 / (HID + 1)))
        linear_coef = jax.random.uniform(ks[5], (HID, 1), minval=-lim3, maxval=lim3, dtype=jnp.float32)
        return {'hidden_atom_emb': hidden_atom_emb, 'edge_emb': edge_emb, 'W1': W1, 'b1': b1, 'W2': W2, 'b2': b2, 'linear_coef': linear_coef, 'edge_list': edge_list}
    _L0_gnn_all = _L0_gnn_setup()
    _L0_gnn_in = {k: v for k, v in _L0_gnn_all.items() if k in ('W1', 'b1', 'W2', 'b2', 'linear_coef')}
    del _L0_gnn_all
    return {'x': x, 'src': src, 'dst': dst, 'edge_attr_64': edge_attr_64, 'L0_gnn_W1': _L0_gnn_in['W1'], 'L0_gnn_b1': _L0_gnn_in['b1'], 'L0_gnn_W2': _L0_gnn_in['W2'], 'L0_gnn_b2': _L0_gnn_in['b2'], 'L0_gnn_linear_coef': _L0_gnn_in['linear_coef']}

def reference(x, src, dst, edge_attr_64, L0_gnn_W1, L0_gnn_b1, L0_gnn_W2, L0_gnn_b2, L0_gnn_linear_coef):
    import jax
    import jax.numpy as jnp

    def _L0_gnn_ref(hidden_atom_emb, edge_emb, W1, b1, W2, b2, linear_coef, edge_list):
        import jax, jax.numpy as jnp
        import numpy as np
        N_NODES = 6250
        N_EDGES = 100000
        EDGE_DIM = 64
        HID = 64
        hidden_edge_emb = jnp.tanh(edge_emb @ W1 + b1) @ W2 + b2
        msg = hidden_atom_emb[edge_list[:, 1]] * hidden_edge_emb
        attn = jnp.exp(msg @ linear_coef)
        dest = edge_list[:, 0]
        n = hidden_atom_emb.shape[0]
        num = jax.ops.segment_sum(msg * attn, dest, num_segments=n)
        den = jax.ops.segment_sum(jnp.broadcast_to(attn, msg.shape), dest, num_segments=n)
        return jnp.where(den > 0, num / den, num)
    edge_index_t = jnp.stack([src, dst], axis=1)
    x = _layernorm(x + _L0_gnn_ref(x, edge_attr_64, L0_gnn_W1, L0_gnn_b1, L0_gnn_W2, L0_gnn_b2, L0_gnn_linear_coef, edge_index_t), axis=-1)
    return x

_drawn_inputs = setup_inputs


def setup_inputs(seed=0):
    import zlib

    import numpy as np

    out = dict(_drawn_inputs(seed))
    spreads = {'L0_gnn_b1': (0.0, 0.1), 'L0_gnn_b2': (0.0, 0.1)}
    factors = {}
    for name, (base, spread) in spreads.items():
        noise = np.random.default_rng([zlib.crc32(name.encode()), seed]).standard_normal(out[name].shape)
        drawn = base * np.exp(spread * noise) if base else spread * noise
        out[name] = jnp.asarray(drawn.astype(out[name].dtype))
    for name, factor in factors.items():
        out[name] = (out[name] * factor).astype(out[name].dtype)
    return out
```

```python
from contextlib import ExitStack

import concourse.bass as bass
from concourse import mybir

ALU = mybir.AluOpType
ACT = mybir.ActivationFunctionType
AX = mybir.AxisListType
F32 = mybir.dt.float32
BF16 = mybir.dt.bfloat16
I32 = mybir.dt.int32
U32 = mybir.dt.uint32

P = 128
D = 64
J = 4
GE = P * J
ROW = 68
ONE, ATT, LOW = D, D + 1, D + 2
ACC = D + 1
BIG = float(1 << 18)
PASSES = 2
CAP = 9
FULL = 7
UNROLL = 4


def node_sums_kernel(nc, x, src, dst, edge, W1, b1, W2, b2, coef, out):
    N = x.shape[0]
    E = src.shape[0]
    NG = -(-E // GE)
    EL = E - (NG - 1) * GE
    PL = EL // J
    NB = -(-N // P)
    NL = N - (NB - 1) * P
    NBK = NB + 1
    G1 = -(-NG // PASSES // UNROLL) * UNROLL
    T = -(-NG * J // 16) * 16
    GT = -(-NG // P)
    GREST = NG - 1 - (GT - 1) * P
    REGION = CAP * P
    PART = NB * REGION
    DUMP = PASSES * PART
    ROWS = DUMP + GE
    XB = N - P
    NHI, NLO = 8, 16
    assert EL % J == 0 and NB <= NHI * NLO and ROWS < BIG and GREST >= 0 and D * 2 == P
    assert G1 * J % 16 == 0 and T - NG * J < GE * J and (NG - G1) % UNROLL == 3

    rows_dram = nc.dram_tensor("scattered_rows", [ROWS, ROW], F32).ap()
    rel_dram = nc.dram_tensor("relative_dst", [GT * P, GE], BF16).ap()
    base_dram = nc.dram_tensor("window_bases", [1, GT * P], I32).ap()
    GP = 125
    GN = E // GP
    assert GN * GP == E
    sums_dram = nc.dram_tensor("general_sums", [NB * P + P, ACC], F32).ap()

    with ExitStack() as ctx:
        def sb(name, shape, dt=F32):
            return ctx.enter_context(nc.sbuf_tensor(name, shape, dt))

        def sem(name):
            return ctx.enter_context(nc.semaphore(name))

        bank = [ctx.enter_context(nc.psum_tensor(f"bank{b}", [P, 512], F32)) for b in range(8)]

        iota_i = sb("iota_i", [P, P], I32)
        part_i = sb("part_i", [P, 1], I32)
        digit_i = sb("digit_i", [P, 2], I32)
        iota_n = sb("iota_n", [P, P])
        part = sb("part", [P, 1])
        digit = sb("digit", [P, 2])
        iota_b = sb("iota_b", [P, P], BF16)
        ident = sb("ident", [P, P])
        ones_f = sb("ones_f", [P, P])
        ones_b = sb("ones_b", [P, P], BF16)
        earlier = sb("earlier", [P, P])
        count_own = sb("count_own", [P, P], BF16)
        count_rest = sb("count_rest", [P, P], BF16)
        drop_own = sb("drop_own", [P, P], BF16)
        later_f = sb("later_f", [P, P])
        W1d = sb("W1d", [P, P])
        W2d = sb("W2d", [P, P])
        b1c = sb("b1c", [P, 1])
        b2f = sb("b2f", [3, J * D])
        b2r = sb("b2r", [3, J * D])
        b2s = sb("b2s", [3, J * D])
        b2h = sb("b2h", [3, J * D], BF16)
        b2p = sb("b2p", [3, J * D], BF16)
        coef_b = sb("coef_b", [P, D])
        start_i = sb("start_i", [1, NBK], I32)
        start_f = sb("start_f", [1, PASSES, NBK])
        zero = sb("zero", [P, CAP * ROW])

        src4 = sb("src4", [P, GT, GE], I32)
        dst4 = sb("dst4", [P, GT, GE], I32)
        src4f = sb("src4f", [P, GT, GE])
        dst4f = sb("dst4f", [P, GT, GE])
        base_f = sb("base_f", [P, GT])
        base_i = sb("base_i", [P, GT], I32)
        rel = sb("rel", [P, GT, GE], BF16)
        srcT = sb("srcT", [P, T], I32)
        blkT = sb("blkT", [P, T], I32)
        block_b = sb("block_b", [P, T], BF16)
        low_f = sb("low_f", [P, T])
        digit_b = sb("digit_b", [P, 2, T], BF16)
        hist_m = sb("hist_m", [P, PASSES, NLO, NLO])
        hist_r = sb("hist_r", [P, PASSES, NLO])
        hist_x = sb("hist_x", [P, PASSES, NHI, NLO])
        maskt = sb("maskt", [P, NLO])
        maskk = sb("maskk", [P, NHI])
        viol = sb("viol", [P, 8])
        flag_i = sb("flag_i", [1, 1], I32)
        base_row = sb("base_row", [1, GT * P], I32)

        shared = sb("shared", [P, (NHI + NLO) * T // 2])
        hot_hi = shared[:, 0:NHI * T // 2].bitcast(BF16).rearrange("p (t k) -> p t k", k=NHI)
        hot_lo = shared[:, NHI * T // 2:(NHI + NLO) * T // 2].bitcast(BF16).rearrange("p (k t) -> p k t", t=T)
        acc = shared[:, 0:NB * ACC].rearrange("p (b f) -> p b f", f=ACC)
        xres = shared[:, NB * ACC:NB * (ACC + D)].rearrange("p (b f) -> p b f", f=D)

        ed = sb("ed", [P, UNROLL, J * D])
        win = sb("win", [P, UNROLL, D])
        rel_row = sb("rel_row", [1, 2, 2 * GE], BF16)
        hot = sb("hot", [P, 2, J, NBK], BF16)
        slot = sb("slot", [P, UNROLL, J], U32)
        onehot = sb("onehot", [P, 2, GE])
        edT = sb("edT", [P, 2, 2 * P])
        h1 = sb("h1", [P, 2, 2 * P])
        xg = sb("xg", [P, 2, J, D])
        weighted = sb("weighted", [P, J, D])
        score = sb("score", [P, 2, J])
        rows = sb("rows", [P, UNROLL, J, ROW])
        back = sb("back", [P, 2, CAP, ROW])
        pick = sb("pick", [P, 2, CAP, P])
        FB = 7
        den = sb("den", [P, NB, 1])
        fix = sb("fix", [P, NB, 1])
        y = sb("y", [P, 2, FB, D])
        sq = sb("sq", [P, 2, FB, D])
        mean = sb("mean", [P, 2, FB, 1])
        var = sb("var", [P, 2, FB, 1])
        g_ed = sb("g_ed", [P, D])
        g_src = sb("g_src", [P, 1], I32)
        g_dst = sb("g_dst", [P, 1], I32)
        g_srcf = sb("g_srcf", [P, 1])
        g_srcb = sb("g_srcb", [P, P])
        g_x = sb("g_x", [P, D])
        g_sum = sb("g_sum", [P, ACC])
        g_edT = sb("g_edT", [D, P])
        g_h1 = sb("g_h1", [D, P])
        g_same = sb("g_same", [P, P])
        g_prev = sb("g_prev", [P, P])
        g_n = sb("g_n", [P, 4])
        g_msg = sb("g_msg", [P, ACC])
        g_t = sb("g_t", [P, D])
        g_to = sb("g_to", [P, 1], U32)

        psT, psH1, psH2, psRel, psX, psRank, psSum = bank[0], bank[1], bank[2], bank[3], bank[4], bank[5], bank[6]

        iotas = sem("iotas")
        consts = sem("consts")
        weights_in = sem("weights_in")
        matrices_in = sem("matrices_in")
        memset_done = sem("memset_done")
        src_in = sem("src_in")
        dst_in = sem("dst_in")
        dst_end_in = sem("dst_end_in")
        src_float = sem("src_float")
        dst_float = sem("dst_float")
        dst_rel = sem("dst_rel")
        src_turned = sem("src_turned")
        src_back = sem("src_back")
        digits = sem("digits")
        hist_made = sem("hist_made")
        hist_read = sem("hist_read")
        hist_ready = sem("hist_ready")
        counts_made = sem("counts_made")
        viol_ready = sem("viol_ready")
        viol_made = sem("viol_made")
        flag_ready = sem("flag_ready")
        rel_out = sem("rel_out")
        base_in = sem("base_in")
        zeroed = sem("zeroed")
        dve_step = sem("dve_step")
        b2_ready = sem("b2_ready")
        ed_in = [sem(f"ed_in{u}") for u in range(UNROLL)]
        win_in = [sem(f"win_in{u}") for u in range(UNROLL)]
        rel_in = [sem(f"rel_in{q}") for q in range(2)]
        edT_made = sem("edT_made")
        edT_ready = sem("edT_ready")
        h1_made = sem("h1_made")
        h1_ready = sem("h1_ready")
        h2_made = sem("h2_made")
        rel_spread = sem("rel_spread")
        onehot_ready = sem("onehot_ready")
        x_made = sem("x_made")
        x_ready = sem("x_ready")
        hot_ready = sem("hot_ready")
        rank_made = sem("rank_made")
        slot_ready = sem("slot_ready")
        counted = sem("counted")
        msg_ready = sem("msg_ready")
        weighted_ready = sem("weighted_ready")
        score_ready = sem("score_ready")
        rows_ready = sem("rows_ready")
        scattered = [sem(f"scattered{u}") for u in range(UNROLL)]
        back_in = [sem(f"back_in{q}") for q in range(2)]
        pick_ready = sem("pick_ready")
        sum_made = sem("sum_made")
        sum_kept = sem("sum_kept")
        pool_event = sem("pool_event")
        pe_event = sem("pe_event")
        g_zeroed = sem("g_zeroed")
        g_in = sem("g_in")
        g_gathered = sem("g_gathered")
        g_pe = sem("g_pe")
        g_act = sem("g_act")
        g_dve = sem("g_dve")
        g_done = sem("g_done")
        g_back = sem("g_back")
        acc_zero = sem("acc_zero")
        xres_in = sem("xres_in")
        node_scaled = sem("node_scaled")
        var_ready = sem("var_ready")
        std_ready = sem("std_ready")
        y_ready = sem("y_ready")
        out_done = [sem(f"out_done{q}") for q in range(2)]

        def late(eng, semaphore, value):
            if not (isinstance(value, int) and value <= 0):
                eng.wait_ge(semaphore, value)

        def uses(s, k):
            return s // k

        def real(s):
            return not isinstance(s, int) or 0 <= s < NG

        FULL_IT = (NG - G1) // UNROLL
        IT1 = G1 // UNROLL

        def run_steps(eng, step, block):
            for u in range(UNROLL):
                step(u, u, 0)
            with eng.Fori(1, IT1) as i:
                for u in range(UNROLL):
                    step(i * UNROLL + u, u, i)
            for u in range(UNROLL):
                step(G1 + u, u, IT1)
            for u in range(UNROLL):
                step(G1 + UNROLL + u, u, IT1 + 1)
                if u % 2 == 1:
                    block(u // 2, u // 2, 0, 0)
            with eng.Fori(1, FULL_IT - 1) as i:
                for u in range(UNROLL):
                    step(i * UNROLL + (G1 + UNROLL + u), u, i + (IT1 + 1))
                    if u % 2 == 1:
                        block(i * 2 + u // 2, u // 2, i, 0)
            s0 = G1 + UNROLL * FULL_IT
            b = 2 * (FULL_IT - 1)
            for s in range(s0, NG + 2):
                step(s, s % UNROLL, s // UNROLL)
                if b < NB:
                    block(b, b % 2, b // 2, 0)
                    b += 1
            while b < NB:
                block(b, b % 2, b // 2, 0)
                b += 1

        def run_tail(eng, block):
            block(0, 0, NB // 2, 1)
            block(1, 1, NB // 2, 1)
            with eng.Fori(1, NB // 2) as i:
                block(i * 2, 0, i + NB // 2, 1)
                block(i * 2 + 1, 1, i + NB // 2, 1)

        block_ = ctx.enter_context(nc.Block())

        @block_.sync
        def _(sp):
            sp.wait_ge(memset_done, 2)
            for idx, tile, done in ((src, src4, src_in), (dst, dst4, dst_in)):
                whole = (GT - 1) * P * GE
                sp.dma_start(tile[:, 0:GT - 1, :], idx[0:whole].rearrange("(t p e) -> p t e", p=P, e=GE)).then_inc(done, 16)
                sp.dma_start(tile[0:GREST, GT - 1, :], idx[whole:(NG - 1) * GE].rearrange("(p e) -> p e", e=GE)).then_inc(done, 16)
                sp.dma_start(tile[GREST:GREST + 1, GT - 1, 0:EL], idx[(NG - 1) * GE:E].rearrange("(p e) -> p e", p=1)).then_inc(done, 16)
            sp.dma_start(dst4[GREST:GREST + 1, GT - 1, EL:GE], dst[E - (GE - EL):E].rearrange("(p e) -> p e", p=1)).then_inc(dst_in, 16)
            sp.wait_ge(dst_rel, 2)
            sp.dma_start(rel_dram.rearrange("(t p) e -> p t e", p=P), rel[:, :, :]).then_inc(rel_out, 16)
            with nc.allow_non_contiguous_dma(reason="512 numbers"):
                sp.dma_start(base_dram.rearrange("a (t p) -> p (a t)", p=P), base_i[:, :]).then_inc(rel_out, 16)
            sp.wait_ge(rel_out, 32)
            sp.dma_start(base_row[:, :], base_dram).then_inc(base_in, 16)
            sp.wait_ge(base_in, 16)
            sp.wait_ge(flag_ready, 1)
            general = sp.value_load(flag_i[0:1, 0:1], min_val=0, max_val=1)

            def step(s, u, i):
                if not real(s):
                    return
                last = isinstance(s, int) and s == NG - 1
                np_ = PL if last else P
                if u == 0:
                    n = min(UNROLL, NG - s) if isinstance(s, int) else UNROLL
                    step.bases = nc.values_load_multi_w_load_instructions(
                        base_row[0:1, bass.ds(s, n)], engines=[mybir.EngineType.SP], min_val=0, max_val=XB)[1]
                late(sp, edT_made, s - UNROLL + 1)
                sp.dma_start(ed[0:np_, u, :], edge[bass.ds(s * GE, np_ * J), :].rearrange("(p j) f -> p (j f)", j=J)).then_inc(ed_in[u], 16)
                late(sp, x_made, s - UNROLL + 1)
                sp.dma_start(win[:, u, :], x[bass.ds(step.bases[u], P), :]).then_inc(win_in[u], 16)
                if u % 2 == 1 or last:
                    e0, n = (s, 1) if last else (s - 1, 2)
                    sp.dma_start(rel_row[0:1, u // 2, 0:n * GE],
                                 rel_dram[bass.ds(e0, n), :].rearrange("g e -> (g e)").rearrange("(a e) -> a e", a=1)).then_inc(rel_in[u // 2], 16)

            def block(b, q, i, part_):
                if part_ == 0:
                    for u in range(UNROLL):
                        sp.wait_ge(scattered[u], 16 * J * IT1)
                use = (2 * i + q) if isinstance(i, int) else i * 2 + q
                late(sp, sum_made, use - 1)
                r0 = (b * REGION) + part_ * PART
                sp.dma_start(back[:, q, :, :], rows_dram[bass.ds(r0, REGION), :].rearrange("(p k) f -> p k f", k=CAP)).then_inc(back_in[q], 16)

            with sp.If(general < 1):
                sp.wait_ge(iotas, 6)
                run_steps(sp, step, block)
                for u in range(UNROLL):
                    sp.wait_ge(scattered[u], 16 * J * len(range(u, NG, UNROLL)))
                run_tail(sp, block)
            with sp.Else():
                sp.wait_ge(memset_done, 3)
                for c in range(2):
                    sp.dma_start(sums_dram[c * NB * P // 2:(c + 1) * NB * P // 2, :].rearrange("(p k) f -> p (k f)", p=NB * P // 2 // 49),
                                 xres[0:P, :, :].rearrange("p b f -> p (b f)")[:, 0:49 * ACC]).then_inc(g_zeroed, 16)
                sp.dma_start(sums_dram[NB * P:NB * P + P, :], xres[:, 0:2, :].rearrange("p b f -> p (b f)")[:, 0:ACC]).then_inc(g_zeroed, 16)
                with sp.Fori(0, GN) as i:
                    sp.wait_ge(g_done, i * 16)
                    sp.dma_start(g_ed[0:GP, :], edge[bass.ds(i * GP, GP), :]).then_inc(g_in, 16)
                    sp.dma_start(g_src[0:GP, :], src[bass.ds(i * GP, GP)].rearrange("(p a) -> p a", a=1)).then_inc(g_in, 16)
                    sp.dma_start(g_dst[0:GP, :], dst[bass.ds(i * GP, GP)].rearrange("(p a) -> p a", a=1)).then_inc(g_in, 16)
                sp.wait_ge(g_done, GN * 16)
                sp.wait_ge(acc_zero, 1)
                sp.dma_start(acc[:, :, :], sums_dram[0:NB * P, :].rearrange("(b p) f -> p b f", p=P)).then_inc(g_back, 16)
            sp.wait_ge(acc_zero, 2)
            sp.dma_start(xres[:, 0:NB - 1, :], x[0:(NB - 1) * P, :].rearrange("(b p) f -> p b f", p=P)).then_inc(xres_in, 16)
            sp.dma_start(xres[0:NL, NB - 1, :], x[(NB - 1) * P:N, :]).then_inc(xres_in, 16)
            for n in range(NB // FB):
                sp.wait_ge(y_ready, n + 1)
                b = n * FB
                if n < NB // FB - 1:
                    sp.dma_start(out[b * P:(b + FB) * P, :].rearrange("(b p) f -> p b f", p=P), y[:, n % 2, :, :]).then_inc(out_done[n % 2], 16)
                else:
                    sp.dma_start(out[b * P:(b + FB - 1) * P, :].rearrange("(b p) f -> p b f", p=P), y[:, n % 2, 0:FB - 1, :]).then_inc(out_done[n % 2], 16)
                    sp.dma_start(out[(NB - 1) * P:N, :], y[0:NL, n % 2, FB - 1, :]).then_inc(out_done[n % 2], 16)
            sp.wait_ge(out_done[0], 16 * (NB // FB // 2))
            sp.wait_ge(out_done[1], 16 * (NB // FB // 2 + 1))

        @block_.gpsimd
        def _(pool):
            nc.gpsimd.iota(iota_i[:, :], [[1, P]], base=0, channel_multiplier=0).then_inc(iotas, 1)
            nc.gpsimd.iota(part_i[:, :], [[1, 1]], base=0, channel_multiplier=1).then_inc(iotas, 1)
            nc.gpsimd.iota(start_i[0:1, :], [[REGION, NBK]], base=0, channel_multiplier=0).then_inc(iotas, 1)
            nc.gpsimd.memset(zero[:, :], 0.0).then_inc(iotas, 1)
            nc.gpsimd.memset(rows[:, :, :, :], 1.0).then_inc(iotas, 1)
            nc.gpsimd.memset(ed[:, :, :], 0.0).then_inc(iotas, 1)
            pool.wait_ge(flag_ready, 1)
            general = pool.value_load(flag_i[0:1, 0:1], min_val=0, max_val=1)

            def step(s, u, i):
                if isinstance(s, int) and s < 2:
                    return
                v = (u + 2) % UNROLL
                pool.wait_ge(rows_ready, s - 1)
                pool.sem_inc(pool_event, 1)
                for j in range(J):
                    nc.gpsimd.indirect_dma_start(
                        out=rows_dram[:, :], out_offset=bass.IndirectOffsetOnAxis(ap=slot[:, v, j:j + 1], axis=0),
                        in_=rows[:, v, j, :], in_offset=None).then_inc(scattered[v], 16)

            with pool.If(general < 1):
                pool.wait_ge(zeroed, 32 * PASSES)
                run_steps(pool, step, lambda *a: None)
            with pool.Else():
                pool.wait_ge(g_zeroed, 48)
                with pool.Fori(0, GN) as i:
                    pool.wait_ge(g_in, i * 48 + 48)
                    pool.sem_inc(pool_event, 1)
                    nc.gpsimd.indirect_dma_start(out=g_x[0:GP, :], out_offset=None, in_=x[:, :],
                                                 in_offset=bass.IndirectOffsetOnAxis(ap=g_dst[0:GP, 0:1].bitcast(U32), axis=0)).then_inc(g_gathered, 16)
                    nc.gpsimd.indirect_dma_start(out=g_sum[0:GP, :], out_offset=None, in_=sums_dram[:, :],
                                                 in_offset=bass.IndirectOffsetOnAxis(ap=g_src[0:GP, 0:1].bitcast(U32), axis=0)).then_inc(g_gathered, 16)
                    pool.wait_ge(g_dve, i * 9 + 9)
                    pool.sem_inc(pool_event, 1)
                    nc.gpsimd.indirect_dma_start(out=sums_dram[:, :], out_offset=bass.IndirectOffsetOnAxis(ap=g_to[0:GP, 0:1], axis=0),
                                                 in_=g_msg[0:GP, :], in_offset=None).then_inc(g_done, 16)
                pool.wait_ge(g_done, GN * 16)

        @block_.tensor
        def _(pe):
            pe.wait_ge(src_float, 1)
            pe.wait_ge(consts, 1)
            for t in range(GT):
                n = min(P, T // J - t * P)
                for j in range(J):
                    m = pe.transpose(bank[t][:, j * P:j * P + n], src4f[0:n, t, j::J], ident[0:n, 0:n])
                m.then_inc(src_turned, 1)
            pe.wait_ge(digits, 1)
            for c, (t0, t1) in enumerate(((0, G1 * J), (G1 * J, T))):
                for t in range(t0, t1, 16):
                    m = pe.matmul(bank[4][:, c * 256:c * 256 + 256], hot_hi[:, t:t + 16, :].rearrange("p t k -> p (t k)"),
                                  hot_lo[:, :, t:t + 16], start=(t == t0), stop=(t + 16 >= t1))
            m.then_inc(hist_made, 1)
            pe.wait_ge(hist_ready, 1)
            pe.matmul(bank[5][:, 0:PASSES * NHI * NLO], ones_f[:, :], hist_x[:, :, :, :], start=True, stop=True).then_inc(counts_made, 1)
            pe.wait_ge(viol_ready, 1)
            pe.matmul(bank[6][:, 0:8], ones_f[:, :], viol[:, :], start=True, stop=True).then_inc(viol_made, 1)
            pe.wait_ge(matrices_in, 16 * 4)
            pe.wait_ge(b2_ready, 1)
            pe.wait_ge(consts, 2)
            pe.wait_ge(flag_ready, 1)
            general = pe.value_load(flag_i[0:1, 0:1], min_val=0, max_val=1)
            rank4 = psRank[:, 0:J * NBK].rearrange("p (j b) -> p j b", j=J)

            def step(s, u, i):
                h = u % 2
                h1_, prev = 1 - h, s - 1
                have, have_prev = real(s), real(s - 1)
                if have_prev and not (isinstance(s, int) and s in (G1,)):
                    pe.wait_ge(slot_ready, s)
                    o = hot[:, h1_, :, :]
                    pe.matmul(psRank[:, 0:J * NBK], drop_own[:, :], o, start=False, stop=False, skip_group_check=True)
                    pe.matmul(psRank[:, 0:J * NBK], count_rest[:, :], o, start=False, stop=False, skip_group_check=True)
                    for j in range(1, J):
                        m = pe.matmul(rank4[:, 0:j, :], ones_b[:, :], o[:, j:j + 1, :].to_broadcast([P, j, NBK]),
                                      start=False, stop=False, skip_group_check=True)
                    m.then_inc(counted, 1)
                if isinstance(s, int) and s in (0, G1):
                    c = 0 if s == 0 else 1
                    if c:
                        pe.wait_ge(slot_ready, s)
                    pe.matmul(rank4, ones_f[0:1, :], start_f[0:1, c:c + 1, :].to_broadcast([1, J, NBK]),
                              start=True, stop=False, skip_group_check=True)
                    if c:
                        pe.matmul(bank[7][0:2, 0:2], ones_b[:, 0:2], ones_b[:, 0:2], start=True, stop=True).then_inc(counted, 1)
                if have:
                    pe.wait_ge(hot_ready, s + 1)
                    o = hot[:, h, :, :]
                    m = pe.matmul(psRank[:, 0:J * NBK], count_own[:, :], o, start=False, stop=False, skip_group_check=True)
                    for j in range(J - 1):
                        m = pe.matmul(rank4[:, j + 1:J, :], ones_b[:, :], o[:, j:j + 1, :].to_broadcast([P, J - 1 - j, NBK]),
                                      start=False, stop=False, skip_group_check=True)
                    m.then_inc(rank_made, 1)
                    pe.wait_ge(ed_in[u], (i + 1) * 16)
                    late(pe, edT_ready, s - 1)
                    for a in range(2):
                        m = pe.transpose(psT[:, h * 256 + a * P:h * 256 + a * P + P], ed[:, u, a * P:a * P + P], ident[:, :])
                    m.then_inc(edT_made, 1)
                    pe.wait_ge(rel_in[u // 2], (i + 1) * 16)
                    late(pe, onehot_ready, s)
                    pe.matmul(psRel[:, :], ones_b[0:1, :], rel_row[0:1, u // 2, h * GE:h * GE + GE],
                              start=True, stop=True).then_inc(rel_spread, 1)
                if have_prev:
                    pe.wait_ge(h1_ready, s)
                    late(pe, msg_ready, s - 2)
                    o = psH2[:, h1_ * 256:h1_ * 256 + 256]
                    pe.matmul(o, ones_b[0:3, :], b2p[:, :], start=True, stop=False)
                    for a in range(2):
                        m = pe.matmul(o[:, a * P:a * P + P], h1[:, h1_, a * P:a * P + P], W2d[:, :], start=False, stop=(a == 1))
                    m.then_inc(h2_made, 1)
                    pe.wait_ge(onehot_ready, s)
                    pe.wait_ge(win_in[(u - 1) % UNROLL], (i + 1) * 16 if u else i * 16)
                    late(pe, x_ready, s - 2)
                    for j in range(J):
                        m = pe.matmul(psX[:, h1_ * 256 + j * D:h1_ * 256 + j * D + D], onehot[:, h1_, j:GE:J],
                                      win[:, (u - 1) % UNROLL, :], start=True, stop=True)
                    m.then_inc(x_made, 1)
                if have:
                    pe.wait_ge(edT_ready, s + 1)
                    late(pe, h1_ready, s - 1)
                    pe.matmul(psH1[:, h * 256:h * 256 + 256], W1d[:, :], edT[:, h, :], start=True, stop=True).then_inc(h1_made, 1)

            def block(b, q, i, part_):
                n = i * 2 + q
                pe.wait_ge(pick_ready, n * CAP + CAP)
                late(pe, sum_kept, n - 1)
                for k in range(CAP):
                    m = pe.matmul(psSum[:, q * P:q * P + ACC], pick[:, q, k, :], back[:, q, k, 0:ACC],
                                  start=(k == 0), stop=(k == CAP - 1))
                m.then_inc(sum_made, 1)

            with pe.If(general < 1):
                run_steps(pe, step, block)
                run_tail(pe, block)
            with pe.Else():
                with pe.Fori(0, GN) as i:
                    pe.wait_ge(g_in, i * 48 + 48)
                    pe.wait_ge(g_dve, i * 9 + 2)
                    pe.sem_inc(pe_event, 1)
                    pe.transpose(psT[0:D, 0:GP], g_ed[0:GP, :], ident[0:GP, 0:GP])
                    pe.transpose(psRel[0:GP, 0:GP], g_srcb[0:GP, 0:GP], ident[0:GP, 0:GP]).then_inc(g_pe, 1)
                    pe.wait_ge(g_act, i * 3 + 1)
                    pe.sem_inc(pe_event, 1)
                    pe.matmul(psH1[0:D, 0:GP], W1d[0:D, 0:D], g_edT[:, 0:GP], start=True, stop=True).then_inc(g_pe, 1)
                    pe.wait_ge(g_act, i * 3 + 2)
                    pe.matmul(psH2[0:GP, 0:D], ones_b[0:3, 0:GP], b2p[:, 0:D], start=True, stop=False)
                    pe.matmul(psH2[0:GP, 0:D], g_h1[:, 0:GP], W2d[0:D, 0:D], start=False, stop=True).then_inc(g_pe, 1)
                    pe.wait_ge(g_dve, i * 9 + 8)
                    pe.matmul(psSum[0:GP, 0:ACC], g_same[0:GP, 0:GP], g_msg[0:GP, :], start=True, stop=True).then_inc(g_pe, 1)

        @block_.scalar
        def _(act):
            act.dma_start(b1c[0:D, :], b1.rearrange("(p a) -> p a", a=1)).then_inc(weights_in, 16)
            act.dma_start(b1c[D:P, :], b1.rearrange("(p a) -> p a", a=1)).then_inc(weights_in, 16)
            act.dma_start(coef_b[:, :], coef.rearrange("f a -> a f").to_broadcast([P, D])).then_inc(weights_in, 16)
            act.dma_start(b2f[:, :].rearrange("p (j f) -> p j f", f=D),
                          b2.rearrange("(a c f) -> a c f", a=1, c=1).to_broadcast([3, J, D])).then_inc(weights_in, 16)
            act.wait_ge(consts, 2)
            for W, tile in ((W1, W1d), (W2, W2d)):
                act.dma_start(tile[0:D, 0:D], W).then_inc(matrices_in, 16)
                act.dma_start(tile[D:P, D:P], W).then_inc(matrices_in, 16)
            act.wait_ge(src_in, 48)
            nc.scalar.copy(src4f[:, :, :], src4[:, :, :]).then_inc(src_float, 1)
            act.wait_ge(dst_in, 64)
            nc.scalar.copy(dst4f[:, :, :], dst4[:, :, :]).then_inc(dst_float, 1)
            for t in range(GT):
                n = min(P, T // J - t * P)
                act.wait_ge(src_turned, t + 1)
                nc.scalar.copy(srcT[:, t * P * J:t * P * J + n * J].rearrange("p (g j) -> p j g", j=J),
                               bank[t][:, :].rearrange("p (j g) -> p j g", j=J)[:, :, 0:n]).then_inc(src_back, 1)
            act.wait_ge(flag_ready, 1)
            general = act.value_load(flag_i[0:1, 0:1], min_val=0, max_val=1)

            def clear_ends():
                act.wait_ge(iotas, 4)
                for c in range(PASSES):
                    act.dma_start(
                        rows_dram[c * PART:(c + 1) * PART, :].rearrange("(b r) f -> b (r f)", b=NB)[:, FULL * P * ROW:].rearrange("b (p f) -> p b f", p=P),
                        zero[:, 0:(CAP - FULL) * ROW].rearrange("p (a f) -> p a f", a=1).to_broadcast([P, NB, (CAP - FULL) * ROW])).then_inc(zeroed, 16)
                    r0 = c * PART + (NB - 1) * REGION
                    act.dma_start(rows_dram[r0:r0 + FULL * P, :].rearrange("(p k) f -> p (k f)", p=P),
                                  zero[:, 0:FULL * ROW]).then_inc(zeroed, 16)

            def step(s, u, i):
                h = u % 2
                if real(s):
                    act.wait_ge(edT_made, s + 1)
                    late(act, h1_made, s - 1)
                    nc.scalar.copy(edT[:, h, :], psT[:, h * 256:h * 256 + 256]).then_inc(edT_ready, 1)
                if real(s - 1):
                    act.wait_ge(x_made, s)
                    late(act, msg_ready, s - 2)
                    nc.scalar.copy(xg[:, 1 - h, :, :], psX[:, (1 - h) * 256:(1 - h) * 256 + 256]).then_inc(x_ready, 1)
                if real(s - 2):
                    v = (u + 2) % UNROLL
                    act.wait_ge(score_ready, s - 1)
                    nc.scalar.copy(rows[:, v, :, LOW], low_f[:, bass.ds((s - 2) * J, J)])
                    nc.scalar.activation(rows[:, v, :, ATT], score[:, h, :], ACT.Exp).then_inc(rows_ready, 1)
                if real(s):
                    act.wait_ge(h1_made, s + 1)
                    late(act, h2_made, s - 1)
                    nc.scalar.activation(h1[:, h, :], psH1[:, h * 256:h * 256 + 256], ACT.Tanh, bias=b1c[:, 0:1]).then_inc(h1_ready, 1)

            def block(b, q, i, part_):
                if part_ == 0:
                    act.wait_ge(sum_made, i * 2 + q + 1)
                    nc.scalar.copy(acc[:, bass.ds(b, 1), :], psSum[:, q * P:q * P + ACC]).then_inc(sum_kept, 1)

            with act.If(general < 1):
                clear_ends()
                act.wait_ge(weights_in, 16 * 4)
                act.wait_ge(iotas, 6)
                run_steps(act, step, block)
            with act.Else():
                act.wait_ge(weights_in, 16 * 4)
                with act.Fori(0, GN) as i:
                    act.wait_ge(g_pe, i * 4 + 1)
                    nc.scalar.copy(g_edT[:, 0:GP], psT[0:D, 0:GP]).then_inc(g_act, 1)
                    act.wait_ge(g_pe, i * 4 + 2)
                    nc.scalar.activation(g_h1[:, 0:GP], psH1[0:D, 0:GP], ACT.Tanh, bias=b1c[0:D, 0:1]).then_inc(g_act, 1)
                    act.wait_ge(g_dve, i * 9 + 7)
                    nc.scalar.activation(g_n[0:GP, 2:3], g_n[0:GP, 1:2], ACT.Exp).then_inc(g_act, 1)
            for n in range(NB // FB):
                act.wait_ge(var_ready, n + 1)
                nc.scalar.activation(var[:, n % 2, :, :], var[:, n % 2, :, :], ACT.Sqrt).then_inc(std_ready, 1)

        @block_.vector
        def _(dve):
            at = [0]

            def link(ins):
                at[0] += 1
                ins.then_inc(dve_step, 1)
                dve.wait_ge(dve_step, at[0])

            nc.vector.memset(src4[:, :, :], NB * P).then_inc(memset_done, 1)
            nc.vector.memset(dst4[:, :, :], 0).then_inc(memset_done, 1)
            nc.vector.memset(W1d[:, :], 0.0)
            nc.vector.memset(W2d[:, :], 0.0)
            nc.vector.memset(ones_f[:, :], 1.0)
            nc.vector.memset(ones_b[:, :], 1.0)
            dve.wait_ge(iotas, 3)
            nc.vector.tensor_copy(iota_n[:, :], iota_i[:, :])
            link(nc.vector.tensor_copy(part[:, :], part_i[:, :]))
            nc.vector.tensor_scalar(ident[:, :], iota_n[:, :], part[:, 0:1], None, ALU.is_equal).then_inc(consts, 1)
            nc.vector.tensor_copy(iota_b[:, :], iota_n[:, :])
            nc.vector.tensor_scalar(earlier[:, :], iota_n[:, :], part[:, 0:1], None, ALU.is_gt)
            nc.vector.tensor_scalar(later_f[:, :], iota_n[:, :], part[:, 0:1], None, ALU.is_lt)
            nc.vector.tensor_scalar(count_rest[:, :], iota_n[:, :], part[:, 0:1], None, ALU.is_le)
            nc.vector.tensor_scalar(digit_i[:, 0:1], part_i[:, :], 3, None, ALU.logical_shift_right)
            nc.vector.tensor_scalar(digit_i[:, 1:2], part_i[:, :], NHI - 1, None, ALU.bitwise_and)
            for c in range(PASSES):
                nc.vector.tensor_scalar(start_f[0:1, c, :], start_i[0:1, :], float(c * PART) - BIG, None, ALU.add)
            link(nc.vector.memset(maskt[:, :], 0.0))
            nc.vector.memset(start_f[0:1, 0, NB:NBK], float(DUMP) - BIG)
            nc.vector.memset(start_f[0:1, 1, NB:NBK], float(DUMP) - BIG)
            nc.vector.scalar_tensor_tensor(out=count_own[:, :], in0=ident[:, :], scalar=BIG, in1=earlier[:, :], op0=ALU.mult, op1=ALU.add)
            nc.vector.tensor_scalar(drop_own[:, :], ident[:, :], -BIG, None, ALU.mult)
            link(nc.vector.tensor_copy(digit[:, :], digit_i[:, :]))
            nc.vector.tensor_scalar(maskt[:, :], iota_n[:, 0:NLO], digit[:, 0:1], None, ALU.is_equal)
            nc.vector.tensor_scalar(maskk[:, :], iota_n[:, 0:NHI], digit[:, 1:2], None, ALU.is_equal).then_inc(consts, 1)
            dve.wait_ge(weights_in, 16 * 4)
            link(nc.vector.tensor_copy(b2h[:, :], b2f[:, :]))
            link(nc.vector.tensor_scalar(b2s[:, :], b2h[:, :], ident[0:3, 0:1], None, ALU.mult))
            for k in (1, 2):
                link(nc.vector.tensor_tensor(b2f[:, :], b2f[:, :], b2h[:, :], ALU.subtract))
                link(nc.vector.tensor_copy(b2h[:, :], b2f[:, :]))
                link(nc.vector.tensor_scalar(b2r[:, :], b2h[:, :], ident[0:3, k:k + 1], None, ALU.mult))
                link(nc.vector.tensor_tensor(b2s[:, :], b2s[:, :], b2r[:, :], ALU.add))
            nc.vector.tensor_copy(b2p[:, :], b2s[:, :]).then_inc(b2_ready, 1)
            dve.wait_ge(src_back, GT)
            nc.vector.tensor_scalar(blkT[:, :], srcT[:, :], 7, None, ALU.logical_shift_right)
            link(nc.vector.tensor_scalar(srcT[:, :], srcT[:, :], P - 1, None, ALU.bitwise_and))
            nc.vector.tensor_copy(block_b[:, :], blkT[:, :])
            link(nc.vector.tensor_copy(low_f[:, :], srcT[:, :]))
            link(nc.vector.tensor_scalar(srcT[:, :], blkT[:, :], 4, None, ALU.logical_shift_right))
            link(nc.vector.tensor_copy(digit_b[:, 0, :], srcT[:, :]))
            link(nc.vector.tensor_scalar(blkT[:, :], blkT[:, :], NLO - 1, None, ALU.bitwise_and))
            link(nc.vector.tensor_copy(digit_b[:, 1, :], blkT[:, :]))
            for k in range(NHI):
                nc.vector.tensor_scalar(hot_hi[:, :, k], digit_b[:, 0, :], float(k), None, ALU.is_equal)
            for k in range(NLO):
                m = nc.vector.tensor_scalar(hot_lo[:, k, :], digit_b[:, 1, :], float(k), None, ALU.is_equal)
            m.then_inc(digits, 1)
            dve.wait_ge(dst_float, 1)
            link(nc.vector.tensor_scalar(base_f[:, :], dst4f[:, :, 0], float(XB), None, ALU.min))
            nc.vector.tensor_copy(base_i[:, :], base_f[:, :]).then_inc(dst_rel, 1)
            for t in range(GT):
                m = nc.vector.tensor_scalar(dst4f[:, t, :], dst4f[:, t, :], base_f[:, t:t + 1], None, ALU.subtract)
            link(m)
            nc.vector.tensor_copy(rel[:, :, :], dst4f[:, :, :]).then_inc(dst_rel, 1)
            nc.vector.tensor_reduce(viol[:, 4:5], dst4f[:, :, :], AX.XY, ALU.max)
            link(nc.vector.tensor_reduce(viol[:, 5:6], dst4f[:, :, :], AX.XY, ALU.min))
            nc.vector.tensor_scalar(viol[:, 4:5], viol[:, 4:5], float(P - 1), None, ALU.is_gt)
            nc.vector.tensor_scalar(viol[:, 5:6], viol[:, 5:6], 0.0, None, ALU.is_lt)
            dve.wait_ge(hist_made, 1)
            link(nc.vector.tensor_tensor(hist_m[:, :, :, :].rearrange("p c l t -> p (c l) t"), bank[4][:, :].rearrange("p (l t) -> p l t", t=NLO),
                                         maskt[:, :].rearrange("p (a t) -> p a t", a=1).to_broadcast([P, PASSES * NLO, NLO]), ALU.mult))
            link(nc.vector.tensor_reduce(hist_r[:, :, :], hist_m[:, :, :, :], AX.X, ALU.add))
            for c in range(PASSES):
                m = nc.vector.tensor_tensor(hist_x[:, c, :, :], hist_r[:, c:c + 1, :].to_broadcast([P, NHI, NLO]),
                                            maskk[:, :].rearrange("p (k a) -> p k a", a=1).to_broadcast([P, NHI, NLO]), ALU.mult)
            m.then_inc(hist_ready, 1)
            dve.wait_ge(counts_made, 1)
            counts = bank[5][:, 0:PASSES * NHI * NLO].rearrange("p (c b) -> p c b", c=PASSES)[:, :, 0:NB]
            nc.vector.tensor_reduce(viol[:, 0:2], counts, AX.X, ALU.max)
            link(nc.vector.tensor_reduce(viol[:, 2:4], counts[:, :, 0:NB - 1], AX.X, ALU.min))
            nc.vector.tensor_scalar(viol[:, 0:2], viol[:, 0:2], float(REGION), None, ALU.is_gt)
            nc.vector.memset(viol[:, 6:8], 0.0)
            nc.vector.tensor_scalar(viol[:, 2:4], viol[:, 2:4], float(FULL * P), None, ALU.is_lt).then_inc(viol_ready, 1)
            dve.wait_ge(viol_made, 1)
            link(nc.vector.tensor_reduce(viol[:, 0:1], bank[6][:, 0:8], AX.X, ALU.max))
            nc.vector.tensor_scalar(flag_i[0:1, 0:1], viol[0:1, 0:1], 0.0, None, ALU.is_gt).then_inc(flag_ready, 1)
            dve.wait_ge(flag_ready, 1)
            general = dve.value_load(flag_i[0:1, 0:1], min_val=0, max_val=1)
            coef_j = coef_b[:, :].rearrange("p (a f) -> p a f", a=1).to_broadcast([P, J, D])
            iota_j = iota_b[:, 0:NBK].rearrange("p (a b) -> p a b", a=1).to_broadcast([P, J, NBK])

            def make_hot(s, u):
                late(dve, counted, s - 1)
                nc.vector.tensor_tensor(hot[:, u % 2, :, :], iota_j,
                                        block_b[:, bass.ds(s * J, J)].rearrange("p (j a) -> p j a", a=1).to_broadcast([P, J, NBK]),
                                        ALU.is_equal).then_inc(hot_ready, 1)

            def step(s, u, i):
                h = u % 2
                if isinstance(s, int) and s == 0:
                    make_hot(0, 0)
                if real(s):
                    dve.wait_ge(rank_made, s + 1)
                    late(dve, scattered[u], i * (16 * J))
                    nc.vector.tensor_reduce(slot[:, u, :], psRank[:, 0:J * NBK].rearrange("p (j b) -> p j b", j=J), AX.X, ALU.max).then_inc(slot_ready, 1)
                    dve.wait_ge(rel_spread, s + 1)
                    late(dve, x_made, s - 1)
                    nc.vector.tensor_scalar(onehot[:, h, :], psRel[:, :], part[:, 0:1], None, ALU.is_equal).then_inc(onehot_ready, 1)
                if real(s - 1):
                    v = (u - 1) % UNROLL
                    dve.wait_ge(h2_made, s)
                    dve.wait_ge(x_ready, s)
                    nc.vector.tensor_tensor(rows[:, v, :, 0:D], psH2[:, (1 - h) * 256:(1 - h) * 256 + 256].rearrange("p (j f) -> p j f", j=J),
                                            xg[:, 1 - h, :, :], ALU.mult).then_inc(msg_ready, 1)
                if real(s + 1) and not (isinstance(s, int) and s + 1 == NG):
                    make_hot(s + 1, u + 1)
                if real(s - 1):
                    dve.wait_ge(msg_ready, s)
                    late(dve, score_ready, s - 1)
                    nc.vector.tensor_tensor(weighted[:, :, :], rows[:, v, :, 0:D], coef_j, ALU.mult).then_inc(weighted_ready, 1)
                    dve.wait_ge(weighted_ready, s)
                    late(dve, rows_ready, s - 2)
                    nc.vector.tensor_reduce(score[:, 1 - h, :], weighted[:, :, :], AX.X, ALU.add).then_inc(score_ready, 1)

            def block(b, q, i, part_):
                n = i * 2 + q
                dve.wait_ge(back_in[q], (i + 1) * 16)
                late(dve, sum_made, n - 1)
                for k in range(CAP):
                    nc.vector.tensor_scalar(pick[:, q, k, :], iota_n[:, :], back[:, q, k, LOW:LOW + 1], back[:, q, k, ATT:ATT + 1],
                                            ALU.is_equal, ALU.mult).then_inc(pick_ready, 1)
                if part_ == 1:
                    dve.wait_ge(sum_made, n + 1)
                    nc.vector.tensor_tensor(acc[:, bass.ds(b, 1), :], acc[:, bass.ds(b, 1), :],
                                            psSum[:, q * P:q * P + ACC].rearrange("p (a f) -> p a f", a=1), ALU.add).then_inc(sum_kept, 1)

            with dve.If(general < 1):
                dve.wait_ge(iotas, 6)
                run_steps(dve, step, block)
                dve.wait_ge(sum_kept, NB)
                run_tail(dve, block)
                dve.wait_ge(sum_kept, 2 * NB)
                nc.vector.memset(xres[:, NB - 1, :], 0.0).then_inc(acc_zero, 2)
            with dve.Else():
                link2 = nc.vector.memset(shared[:, 0:NB * (ACC + D)], 0.0)
                link2.then_inc(memset_done, 1)
                dve.wait_ge(memset_done, 3)
                with dve.Fori(0, GN) as i:
                    dve.wait_ge(g_in, i * 48 + 48)
                    nc.vector.tensor_copy(g_srcf[0:GP, :], g_src[0:GP, :]).then_inc(g_dve, 1)
                    dve.wait_ge(g_dve, i * 9 + 1)
                    nc.vector.tensor_scalar(g_srcb[0:GP, :], iota_n[0:GP, :], 0.0, g_srcf[0:GP, 0:1], ALU.mult, ALU.add).then_inc(g_dve, 1)
                    dve.wait_ge(g_pe, i * 4 + 1)
                    nc.vector.tensor_scalar(g_same[0:GP, 0:GP], psRel[0:GP, 0:GP], g_srcf[0:GP, 0:1], None, ALU.is_equal).then_inc(g_dve, 1)
                    dve.wait_ge(g_dve, i * 9 + 3)
                    nc.vector.tensor_tensor(g_prev[0:GP, 0:GP], g_same[0:GP, 0:GP], later_f[0:GP, 0:GP], ALU.mult).then_inc(g_dve, 1)
                    dve.wait_ge(g_pe, i * 4 + 3)
                    dve.wait_ge(g_gathered, i * 32 + 32)
                    nc.vector.tensor_tensor(g_msg[0:GP, 0:D], psH2[0:GP, 0:D], g_x[0:GP, :], ALU.mult).then_inc(g_dve, 1)
                    dve.wait_ge(g_dve, i * 9 + 5)
                    nc.vector.tensor_tensor(g_t[0:GP, :], g_msg[0:GP, 0:D], coef_b[0:GP, :], ALU.mult).then_inc(g_dve, 1)
                    dve.wait_ge(g_dve, i * 9 + 6)
                    nc.vector.tensor_reduce(g_n[0:GP, 1:2], g_t[0:GP, :], AX.X, ALU.add).then_inc(g_dve, 1)
                    nc.vector.tensor_reduce(g_n[0:GP, 0:1], g_prev[0:GP, 0:GP], AX.X, ALU.max)
                    dve.wait_ge(g_act, i * 3 + 3)
                    nc.vector.tensor_copy(g_msg[0:GP, D:D + 1], g_n[0:GP, 2:3])
                    nc.vector.tensor_scalar(g_msg[0:GP, 0:D], g_msg[0:GP, 0:D], g_n[0:GP, 2:3], None, ALU.mult).then_inc(g_dve, 1)
                    dve.wait_ge(g_dve, i * 9 + 8)
                    nc.vector.scalar_tensor_tensor(out=g_n[0:GP, 3:4], in0=part[0:GP, :], scalar=float(NB * P), in1=g_srcf[0:GP, :], op0=ALU.add, op1=ALU.subtract)
                    dve.wait_ge(g_pe, i * 4 + 4)
                    nc.vector.tensor_tensor(g_msg[0:GP, :], psSum[0:GP, 0:ACC], g_sum[0:GP, :], ALU.add)
                    dve.drain()
                    nc.vector.scalar_tensor_tensor(out=g_to[0:GP, :], in0=g_n[0:GP, 3:4], scalar=g_n[0:GP, 0:1], in1=g_srcf[0:GP, :], op0=ALU.mult, op1=ALU.add).then_inc(g_dve, 1)
                dve.wait_ge(g_done, GN * 16)
                nc.vector.memset(xres[:, NB - 1, :], 0.0).then_inc(acc_zero, 2)
                dve.wait_ge(g_back, 16)
            base = at[0]
            link(nc.vector.tensor_scalar(fix[:, :, :], acc[:, :, D:D + 1], 0.0, None, ALU.is_le))
            link(nc.vector.tensor_tensor(den[:, :, :], acc[:, :, D:D + 1], fix[:, :, :], ALU.add))
            link(nc.vector.reciprocal(den[:, :, :], den[:, :, :]))
            dve.wait_ge(xres_in, 32)
            for n in range(NB // FB):
                q = n % 2
                b = n * FB
                if n >= 2:
                    dve.wait_ge(out_done[q], 16 * (n // 2))
                link(nc.vector.tensor_tensor(y[:, q, :, :], acc[:, b:b + FB, 0:D], den[:, b:b + FB, :].to_broadcast([P, FB, D]), ALU.mult))
                link(nc.vector.tensor_tensor(y[:, q, :, :], y[:, q, :, :], xres[:, b:b + FB, :], ALU.add))
                link(nc.vector.tensor_reduce(mean[:, q, :, 0], y[:, q, :, :], AX.X, ALU.add))
                link(nc.vector.tensor_scalar(mean[:, q, :, :], mean[:, q, :, :], 1.0 / D, None, ALU.mult))
                link(nc.vector.tensor_tensor(y[:, q, :, :], y[:, q, :, :], mean[:, q, :, :].to_broadcast([P, FB, D]), ALU.subtract))
                link(nc.vector.tensor_tensor(sq[:, q, :, :], y[:, q, :, :], y[:, q, :, :], ALU.mult))
                link(nc.vector.tensor_reduce(var[:, q, :, 0], sq[:, q, :, :], AX.X, ALU.add))
                nc.vector.tensor_scalar(var[:, q, :, :], var[:, q, :, :], 1.0 / D, 1e-5, ALU.mult, ALU.add).then_inc(var_ready, 1)
                dve.wait_ge(std_ready, n + 1)
                link(nc.vector.reciprocal(var[:, q, :, :], var[:, q, :, :]))
                nc.vector.tensor_tensor(y[:, q, :, :], y[:, q, :, :], var[:, q, :, :].to_broadcast([P, FB, D]), ALU.mult).then_inc(y_ready, 1)


_INS = ["x", "src", "dst", "edge_attr_64", "L0_gnn_W1", "L0_gnn_b1", "L0_gnn_W2", "L0_gnn_b2", "L0_gnn_linear_coef"]


def kernel(**inputs):
    import numpy as _np
    import concourse.bacc as _bacc
    from concourse import mybir as _mybir
    from concourse.bass_utils import run_bass_kernel_spmd as _run

    nc = _bacc.Bacc("TRN2", target_bir_lowering=False, num_devices=1)
    arrays, args = {}, []
    for name in _INS:
        a = _np.ascontiguousarray(inputs[name])
        arrays[f"in_{name}"] = a
        args.append(nc.dram_tensor(f"in_{name}", a.shape, _mybir.dt.from_np(a.dtype), kind="ExternalInput").ap())
    shape = inputs["x"].shape
    args.append(nc.dram_tensor("out", shape, _mybir.dt.float32, kind="ExternalOutput").ap())
    node_sums_kernel(nc, *args)
    r = _run(nc, [arrays], core_ids=[0])
    return r.results[0]["out"]
```

```python
from contextlib import ExitStack

import concourse.bass as bass
from concourse import mybir

ALU = mybir.AluOpType
ACT = mybir.ActivationFunctionType
AX = mybir.AxisListType
F32 = mybir.dt.float32
BF16 = mybir.dt.bfloat16
I32 = mybir.dt.int32
U32 = mybir.dt.uint32

P = 128
D = 64
J = 4
GE = P * J
ROW = 66
ATT, LOW = D, D + 1
ACC = D + 1
BIG = float(1 << 18)
PASSES = 2
SHARE = 264
CAP = (12, 6)
FULL = (9, 4)
UNROLL = 4


def node_sums_kernel(nc, x, src, dst, edge, W1, b1, W2, b2, coef, out):
    N = x.shape[0]
    E = src.shape[0]
    NG = -(-E // GE)
    EL = E - (NG - 1) * GE
    PL = EL // J
    NB = -(-N // P)
    NL = N - (NB - 1) * P
    NBK = NB + 1
    G1 = SHARE
    T = -(-NG * J // 16) * 16
    GT = -(-NG // P)
    GREST = NG - 1 - (GT - 1) * P
    PART = (0, NB * CAP[0] * P)
    DUMP = NB * sum(CAP) * P
    ROWS = DUMP + GE
    XB = N - P
    NHI, NLO = 8, 16
    FB = 7
    NF = NB // FB
    assert NF * FB == NB and NF % 2 == 0
    assert EL % J == 0 and NB <= NHI * NLO and ROWS < BIG and GREST >= 0 and D * 2 == P
    assert G1 * J % 16 == 0 and T - NG * J < GE * J and (NG - G1) % UNROLL == 3

    rows_dram = nc.dram_tensor("scattered_rows", [ROWS, ROW], F32).ap()
    rel_dram = nc.dram_tensor("relative_dst", [GT * P, GE], BF16).ap()
    base_dram = nc.dram_tensor("window_bases", [1, GT * P], I32).ap()
    GP = 125
    GN = E // GP
    assert GN * GP == E
    sums_dram = nc.dram_tensor("general_sums", [NB * P + P, ACC], F32).ap()

    with ExitStack() as ctx:
        def sb(name, shape, dt=F32):
            return ctx.enter_context(nc.sbuf_tensor(name, shape, dt))

        def sem(name):
            return ctx.enter_context(nc.semaphore(name))

        bank = [ctx.enter_context(nc.psum_tensor(f"bank{b}", [P, 512], F32)) for b in range(8)]

        iota_i = sb("iota_i", [P, P], I32)
        part_i = sb("part_i", [P, 1], I32)
        digit_i = sb("digit_i", [P, 2], I32)
        iota_n = sb("iota_n", [P, P])
        part = sb("part", [P, 1])
        digit = sb("digit", [P, 2])
        iota_b = sb("iota_b", [P, P], BF16)
        ident = sb("ident", [P, P])
        ones_f = sb("ones_f", [P, P])
        ones_b = sb("ones_b", [P, P], BF16)
        earlier = sb("earlier", [P, P])
        count_own = sb("count_own", [P, P], BF16)
        count_rest = sb("count_rest", [P, P], BF16)
        drop_own = sb("drop_own", [P, P], BF16)
        later_f = sb("later_f", [P, P])
        W1d = sb("W1d", [P, P])
        W2d = sb("W2d", [P, P])
        b1c = sb("b1c", [P, 1])
        b2f = sb("b2f", [3, J * D])
        b2r = sb("b2r", [3, J * D])
        b2s = sb("b2s", [3, J * D])
        b2h = sb("b2h", [3, J * D], BF16)
        b2p = sb("b2p", [3, J * D], BF16)
        coef_b = sb("coef_b", [P, D])
        start_i = sb("start_i", [1, PASSES, NBK], I32)
        start_f = sb("start_f", [1, PASSES, NBK])
        zero = sb("zero", [P, max(FULL) * ROW])

        index_i = sb("index_i", [P, 2, GT, GE], I32)
        index_f = sb("index_f", [P, 2, GT, GE])
        src4, dst4 = index_i[:, 0, :, :], index_i[:, 1, :, :]
        src4f, dst4f = index_f[:, 0, :, :], index_f[:, 1, :, :]
        base_f = sb("base_f", [P, GT])
        base_i = sb("base_i", [P, GT], I32)
        rel = sb("rel", [P, GT, GE], BF16)
        srcT = sb("srcT", [P, T], I32)
        blkT = sb("blkT", [P, T], I32)
        block_b = sb("block_b", [P, T], BF16)
        low_f = sb("low_f", [P, T])
        digit_b = sb("digit_b", [P, 2, T], BF16)
        hist_m = sb("hist_m", [P, PASSES, NLO, NLO])
        hist_r = sb("hist_r", [P, PASSES, NLO])
        hist_x = sb("hist_x", [P, PASSES, NHI, NLO])
        maskt = sb("maskt", [P, NLO])
        maskk = sb("maskk", [P, NHI])
        viol = sb("viol", [P, 8])
        flag_i = sb("flag_i", [1, 1], I32)
        base_row = sb("base_row", [1, GT * P], I32)

        shared = sb("shared", [P, (NHI + NLO) * T // 2])
        hot_hi = shared[:, 0:NHI * T // 2].bitcast(BF16).rearrange("p (t k) -> p t k", k=NHI)
        hot_lo = shared[:, NHI * T // 2:(NHI + NLO) * T // 2].bitcast(BF16).rearrange("p (k t) -> p k t", t=T)
        acc = shared[:, 0:NB * ACC].rearrange("p (b f) -> p b f", f=ACC)
        xres = shared[:, NB * ACC:NB * (ACC + D)].rearrange("p (b f) -> p b f", f=D)

        ed = sb("ed", [P, UNROLL, J * D])
        win = sb("win", [P, UNROLL, D])
        rel_row = sb("rel_row", [1, 2, 2 * GE], BF16)
        hot = sb("hot", [P, 2, J, NBK], BF16)
        slot = sb("slot", [P, UNROLL, J], U32)
        onehot = sb("onehot", [P, 2, GE])
        edT = sb("edT", [P, 2, 2 * P])
        h1 = sb("h1", [P, 2, 2 * P])
        xg = sb("xg", [P, 2, J, D])
        weighted = sb("weighted", [P, J, D])
        score = sb("score", [P, 2, J])
        rows = sb("rows", [P, UNROLL, J, ROW])
        back0 = index_i[:, :, :, :].bitcast(F32).rearrange("p a t e -> p (a t e)")[:, 0:UNROLL * CAP[0] * ROW].rearrange("p (u k f) -> p u k f", u=UNROLL, k=CAP[0])
        back1 = index_f[:, :, :, :].rearrange("p a t e -> p (a t e)")[:, 0:FB * CAP[1] * ROW].rearrange("p (u k f) -> p u k f", u=FB, k=CAP[1])
        pick = sb("pick", [P, 2, CAP[0], P])
        fix = sb("fix", [P, 2, FB, 1])
        den = sb("den", [P, 2, FB, 1])
        y = sb("y", [P, 2, FB, D])
        mean = sb("mean", [P, 2, FB, 1])
        sq = sb("sq", [P, 2, FB, D])
        var = sb("var", [P, 2, FB, 1])
        g_ed = sb("g_ed", [P, D])
        g_src = sb("g_src", [P, 1], I32)
        g_dst = sb("g_dst", [P, 1], I32)
        g_srcf = sb("g_srcf", [P, 1])
        g_srcb = sb("g_srcb", [P, P])
        g_x = sb("g_x", [P, D])
        g_sum = sb("g_sum", [P, ACC])
        g_edT = sb("g_edT", [D, P])
        g_h1 = sb("g_h1", [D, P])
        g_same = sb("g_same", [P, P])
        g_prev = sb("g_prev", [P, P])
        g_n = sb("g_n", [P, 4])
        g_msg = sb("g_msg", [P, ACC])
        g_t = sb("g_t", [P, D])
        g_to = sb("g_to", [P, 1], U32)

        psT, psH1, psH2, psRel, psX, psRank, psSum = bank[0], bank[1], bank[2], bank[3], bank[4], bank[5], bank[6]
        psSums = [bank[6], bank[7]]

        iotas = sem("iotas")
        consts = sem("consts")
        weights_in = sem("weights_in")
        matrices_in = sem("matrices_in")
        memset_done = sem("memset_done")
        src_in = sem("src_in")
        dst_in = sem("dst_in")
        dst_end_in = sem("dst_end_in")
        src_float = sem("src_float")
        dst_float = sem("dst_float")
        dst_rel = sem("dst_rel")
        src_turned = sem("src_turned")
        src_back = sem("src_back")
        digits = sem("digits")
        hist_made = sem("hist_made")
        hist_read = sem("hist_read")
        hist_ready = sem("hist_ready")
        counts_made = sem("counts_made")
        viol_ready = sem("viol_ready")
        viol_made = sem("viol_made")
        flag_ready = sem("flag_ready")
        rel_out = sem("rel_out")
        base_in = sem("base_in")
        zeroed = sem("zeroed")
        dve_step = sem("dve_step")
        b2_ready = sem("b2_ready")
        ed_in = [sem(f"ed_in{u}") for u in range(UNROLL)]
        win_in = [sem(f"win_in{u}") for u in range(UNROLL)]
        rel_in = [sem(f"rel_in{q}") for q in range(2)]
        edT_made = sem("edT_made")
        edT_ready = sem("edT_ready")
        h1_made = sem("h1_made")
        h1_ready = sem("h1_ready")
        h2_made = sem("h2_made")
        rel_spread = sem("rel_spread")
        onehot_ready = sem("onehot_ready")
        x_made = sem("x_made")
        x_ready = sem("x_ready")
        hot_ready = sem("hot_ready")
        rank_made = sem("rank_made")
        slot_ready = sem("slot_ready")
        counted = sem("counted")
        msg_ready = sem("msg_ready")
        weighted_ready = sem("weighted_ready")
        att_ready = sem("att_ready")
        score_ready = sem("score_ready")
        rows_ready = sem("rows_ready")
        scattered = [sem(f"scattered{u}") for u in range(UNROLL)]
        back0_in = [sem(f"back0_in{u}") for u in range(UNROLL)]
        back1_in = [sem(f"back1_in{k}") for k in range(FB)]
        pick_ready = sem("pick_ready")
        sum_made = sem("sum_made")
        sum_kept = sem("sum_kept")
        pool_event = sem("pool_event")
        pe_event = sem("pe_event")
        g_zeroed = sem("g_zeroed")
        g_in = sem("g_in")
        g_gathered = sem("g_gathered")
        g_pe = sem("g_pe")
        g_act = sem("g_act")
        g_dve = sem("g_dve")
        g_done = sem("g_done")
        g_back = sem("g_back")
        xres_free = sem("xres_free")
        xres_in = sem("xres_in")
        sums_ready = sem("sums_ready")
        fixed = sem("fixed")
        den_ready = sem("den_ready")
        y_scaled = sem("y_scaled")
        y_added = sem("y_added")
        y_summed = sem("y_summed")
        sq_summed = sem("sq_summed")
        den_added = sem("den_added")
        mean_ready = sem("mean_ready")
        y_centred = sem("y_centred")
        y_squared = sem("y_squared")
        var_ready = sem("var_ready")
        std_ready = sem("std_ready")
        rstd_ready = sem("rstd_ready")
        y_ready = sem("y_ready")
        out_done = [sem(f"out_done{q}") for q in range(2)]

        def late(eng, semaphore, value):
            if not (isinstance(value, int) and value <= 0):
                eng.wait_ge(semaphore, value)

        def uses(s, k):
            return s // k

        def real(s):
            return not isinstance(s, int) or 0 <= s < NG

        IT1 = G1 // UNROLL
        IT2 = (NG - G1) // UNROLL
        S0 = G1 + UNROLL
        LAST = NG + 2

        def run_steps(eng, step, block, lag):
            def place(s, u, i):
                k = s - S0 - lag
                use = i - S0 // UNROLL + (u - lag) // UNROLL
                if not isinstance(k, int) or 0 <= k < NB:
                    block(k, (u - lag) % UNROLL, use)

            for u in range(UNROLL):
                step(u, u, 0)
            with eng.Fori(1, IT1) as i:
                for u in range(UNROLL):
                    step(i * UNROLL + u, u, i)
            for s in range(G1, G1 + 2 * UNROLL):
                step(s, s % UNROLL, s // UNROLL)
                place(s, s % UNROLL, s // UNROLL)
            n = NB // UNROLL
            with eng.Fori(IT1 + 2, IT1 + 1 + n) as i:
                for u in range(UNROLL):
                    step(i * UNROLL + u, u, i)
                    place(i * UNROLL + u, u, i)
            s1 = (IT1 + 1 + n) * UNROLL
            for s in range(s1, s1 + UNROLL):
                step(s, s % UNROLL, s // UNROLL)
                place(s, s % UNROLL, s // UNROLL)
            with eng.Fori(s1 // UNROLL + 1, NG // UNROLL) as i:
                for u in range(UNROLL):
                    step(i * UNROLL + u, u, i)
            for s in range(NG // UNROLL * UNROLL, LAST):
                step(s, s % UNROLL, s // UNROLL)

        block_ = ctx.enter_context(nc.Block())

        @block_.sync
        def _(sp):
            sp.wait_ge(memset_done, 2)
            for idx, tile, done in ((src, src4, src_in), (dst, dst4, dst_in)):
                whole = (GT - 1) * P * GE
                sp.dma_start(tile[:, 0:GT - 1, :], idx[0:whole].rearrange("(t p e) -> p t e", p=P, e=GE)).then_inc(done, 16)
                sp.dma_start(tile[0:GREST, GT - 1, :], idx[whole:(NG - 1) * GE].rearrange("(p e) -> p e", e=GE)).then_inc(done, 16)
                sp.dma_start(tile[GREST:GREST + 1, GT - 1, 0:EL], idx[(NG - 1) * GE:E].rearrange("(p e) -> p e", p=1)).then_inc(done, 16)
            sp.dma_start(dst4[GREST:GREST + 1, GT - 1, EL:GE], dst[E - (GE - EL):E].rearrange("(p e) -> p e", p=1)).then_inc(dst_in, 16)
            sp.wait_ge(dst_rel, 2)
            sp.dma_start(rel_dram.rearrange("(t p) e -> p t e", p=P), rel[:, :, :]).then_inc(rel_out, 16)
            with nc.allow_non_contiguous_dma(reason="512 numbers"):
                sp.dma_start(base_dram.rearrange("a (t p) -> p (a t)", p=P), base_i[:, :]).then_inc(rel_out, 16)
            sp.wait_ge(rel_out, 32)
            sp.dma_start(base_row[:, :], base_dram).then_inc(base_in, 16)
            sp.wait_ge(base_in, 16)
            sp.wait_ge(flag_ready, 1)
            general = sp.value_load(flag_i[0:1, 0:1], min_val=0, max_val=1)

            def step(s, u, i):
                if not real(s):
                    return
                last = isinstance(s, int) and s == NG - 1
                np_ = PL if last else P
                if u == 0:
                    n = min(UNROLL, NG - s) if isinstance(s, int) else UNROLL
                    step.bases = nc.values_load_multi_w_load_instructions(
                        base_row[0:1, bass.ds(s, n)], engines=[mybir.EngineType.SP], min_val=0, max_val=XB)[1]
                late(sp, edT_made, s - UNROLL + 1)
                sp.dma_start(ed[0:np_, u, :], edge[bass.ds(s * GE, np_ * J), :].rearrange("(p j) f -> p (j f)", j=J)).then_inc(ed_in[u], 16)
                late(sp, x_made, s - UNROLL + 1)
                sp.dma_start(win[:, u, :], x[bass.ds(step.bases[u], P), :]).then_inc(win_in[u], 16)
                if u % 2 == 1 or last:
                    e0, n = (s, 1) if last else (s - 1, 2)
                    sp.dma_start(rel_row[0:1, u // 2, 0:n * GE],
                                 rel_dram[bass.ds(e0, n), :].rearrange("g e -> (g e)").rearrange("(a e) -> a e", a=1)).then_inc(rel_in[u // 2], 16)

            def block(b, u, use):
                for v in range(UNROLL):
                    sp.wait_ge(scattered[v], 16 * J * IT1)
                late(sp, sum_made, b - UNROLL + 1)
                sp.dma_start(back0[:, u, :, :], rows_dram[bass.ds(b * (CAP[0] * P), CAP[0] * P), :].rearrange("(p k) f -> p k f", k=CAP[0])).then_inc(back0_in[u], 16)

            def load_nodes():
                sp.wait_ge(xres_free, 1)
                sp.dma_start(xres[:, 0:NB - 1, :], x[0:(NB - 1) * P, :].rearrange("(b p) f -> p b f", p=P)).then_inc(xres_in, 16)
                sp.dma_start(xres[0:NL, NB - 1, :], x[(NB - 1) * P:N, :]).then_inc(xres_in, 16)

            with sp.If(general < 1):
                sp.wait_ge(iotas, 6)
                run_steps(sp, step, block, 0)
                load_nodes()
                for u in range(UNROLL):
                    sp.wait_ge(scattered[u], 16 * J * len(range(u, NG, UNROLL)))
                for k in range(FB):
                    sp.dma_start(back1[:, k, :, :], rows_dram[PART[1] + k * CAP[1] * P:PART[1] + (k + 1) * CAP[1] * P, :].rearrange("(p k) f -> p k f", k=CAP[1])).then_inc(back1_in[k], 16)
                with sp.Fori(1, NF) as i:
                    for k in range(FB):
                        sp.wait_ge(sum_made, i * FB + (NB + k + 1 - FB))
                        sp.dma_start(back1[:, k, :, :],
                                     rows_dram[bass.ds(i * (FB * CAP[1] * P) + (PART[1] + k * CAP[1] * P), CAP[1] * P), :].rearrange("(p k) f -> p k f", k=CAP[1])).then_inc(back1_in[k], 16)
            with sp.Else():
                sp.wait_ge(memset_done, 3)
                for c in range(2):
                    sp.dma_start(sums_dram[c * NB * P // 2:(c + 1) * NB * P // 2, :].rearrange("(p k) f -> p (k f)", p=NB * P // 2 // 49),
                                 xres[0:P, :, :].rearrange("p b f -> p (b f)")[:, 0:49 * ACC]).then_inc(g_zeroed, 16)
                sp.dma_start(sums_dram[NB * P:NB * P + P, :], xres[:, 0:2, :].rearrange("p b f -> p (b f)")[:, 0:ACC]).then_inc(g_zeroed, 16)
                with sp.Fori(0, GN) as i:
                    sp.wait_ge(g_done, i * 16)
                    sp.dma_start(g_ed[0:GP, :], edge[bass.ds(i * GP, GP), :]).then_inc(g_in, 16)
                    sp.dma_start(g_src[0:GP, :], src[bass.ds(i * GP, GP)].rearrange("(p a) -> p a", a=1)).then_inc(g_in, 16)
                    sp.dma_start(g_dst[0:GP, :], dst[bass.ds(i * GP, GP)].rearrange("(p a) -> p a", a=1)).then_inc(g_in, 16)
                sp.wait_ge(g_done, GN * 16)
                sp.dma_start(acc[:, :, :], sums_dram[0:NB * P, :].rearrange("(b p) f -> p b f", p=P)).then_inc(g_back, 16)
                load_nodes()
        @block_.gpsimd
        def _(pool):
            nc.gpsimd.iota(iota_i[:, :], [[1, P]], base=0, channel_multiplier=0).then_inc(iotas, 1)
            nc.gpsimd.iota(part_i[:, :], [[1, 1]], base=0, channel_multiplier=1).then_inc(iotas, 1)
            for c in range(PASSES):
                nc.gpsimd.iota(start_i[0:1, c, :], [[CAP[c] * P, NBK]], base=PART[c], channel_multiplier=0).then_inc(iotas, 1)
            nc.gpsimd.memset(zero[:, :], 0.0).then_inc(iotas, 1)
            nc.gpsimd.memset(ed[:, :, :], 0.0).then_inc(iotas, 1)
            pool.wait_ge(flag_ready, 1)
            general = pool.value_load(flag_i[0:1, 0:1], min_val=0, max_val=1)

            def step(s, u, i):
                if isinstance(s, int) and s < 2:
                    return
                v = (u + 2) % UNROLL
                pool.wait_ge(rows_ready, s - 1)
                pool.sem_inc(pool_event, 1)
                for j in range(J):
                    nc.gpsimd.indirect_dma_start(
                        out=rows_dram[:, :], out_offset=bass.IndirectOffsetOnAxis(ap=slot[:, v, j:j + 1], axis=0),
                        in_=rows[:, v, j, :], in_offset=None).then_inc(scattered[v], 16)

            def finish_nodes_pool(pool):
                pool.wait_ge(xres_in, 32)
                for n in range(NF):
                    q = n % 2
                    b = n * FB
                    pool.wait_ge(den_ready, n + 1)
                    late(pool, out_done[q], 16 * (n // 2))
                    nc.gpsimd.tensor_tensor(y[:, q, :, :], acc[:, b:b + FB, 0:D], den[:, q, :, :].to_broadcast([P, FB, D]), ALU.mult).then_inc(y_scaled, 1)
                    pool.wait_ge(y_scaled, n + 1)
                    nc.gpsimd.tensor_tensor(y[:, q, :, :], y[:, q, :, :], xres[:, b:b + FB, :], ALU.add).then_inc(y_added, 1)

            with pool.If(general < 1):
                pool.wait_ge(zeroed, 32 * PASSES)
                run_steps(pool, step, lambda *a: None, 0)
                finish_nodes_pool(pool)
            with pool.Else():
                pool.wait_ge(g_zeroed, 48)
                with pool.Fori(0, GN) as i:
                    pool.wait_ge(g_in, i * 48 + 48)
                    pool.sem_inc(pool_event, 1)
                    nc.gpsimd.indirect_dma_start(out=g_x[0:GP, :], out_offset=None, in_=x[:, :],
                                                 in_offset=bass.IndirectOffsetOnAxis(ap=g_dst[0:GP, 0:1].bitcast(U32), axis=0)).then_inc(g_gathered, 16)
                    nc.gpsimd.indirect_dma_start(out=g_sum[0:GP, :], out_offset=None, in_=sums_dram[:, :],
                                                 in_offset=bass.IndirectOffsetOnAxis(ap=g_src[0:GP, 0:1].bitcast(U32), axis=0)).then_inc(g_gathered, 16)
                    pool.wait_ge(g_dve, i * 9 + 9)
                    pool.sem_inc(pool_event, 1)
                    nc.gpsimd.indirect_dma_start(out=sums_dram[:, :], out_offset=bass.IndirectOffsetOnAxis(ap=g_to[0:GP, 0:1], axis=0),
                                                 in_=g_msg[0:GP, :], in_offset=None).then_inc(g_done, 16)
                pool.wait_ge(g_done, GN * 16)
                finish_nodes_pool(pool)

        @block_.tensor
        def _(pe):
            pe.wait_ge(src_float, 1)
            pe.wait_ge(consts, 1)
            for t in range(GT):
                n = min(P, T // J - t * P)
                for j in range(J):
                    m = pe.transpose(bank[t][:, j * P:j * P + n], src4f[0:n, t, j::J], ident[0:n, 0:n])
                m.then_inc(src_turned, 1)
            pe.wait_ge(digits, 1)
            for c, (t0, t1) in enumerate(((0, G1 * J), (G1 * J, T))):
                for t in range(t0, t1, 16):
                    m = pe.matmul(bank[4][:, c * 256:c * 256 + 256], hot_hi[:, t:t + 16, :].rearrange("p t k -> p (t k)"),
                                  hot_lo[:, :, t:t + 16], start=(t == t0), stop=(t + 16 >= t1))
            m.then_inc(hist_made, 1)
            pe.wait_ge(hist_ready, 1)
            pe.matmul(bank[5][:, 0:PASSES * NHI * NLO], ones_f[:, :], hist_x[:, :, :, :], start=True, stop=True).then_inc(counts_made, 1)
            pe.wait_ge(viol_ready, 1)
            pe.matmul(bank[6][:, 0:8], ones_f[:, :], viol[:, :], start=True, stop=True).then_inc(viol_made, 1)
            pe.wait_ge(matrices_in, 16 * 4)
            pe.wait_ge(b2_ready, 1)
            pe.wait_ge(consts, 2)
            pe.wait_ge(flag_ready, 1)
            general = pe.value_load(flag_i[0:1, 0:1], min_val=0, max_val=1)
            rank4 = psRank[:, 0:J * NBK].rearrange("p (j b) -> p j b", j=J)

            def step(s, u, i):
                h = u % 2
                h1_, prev = 1 - h, s - 1
                have, have_prev = real(s), real(s - 1)
                if have_prev and not (isinstance(s, int) and s in (G1,)):
                    pe.wait_ge(slot_ready, s)
                    o = hot[:, h1_, :, :]
                    pe.matmul(psRank[:, 0:J * NBK], drop_own[:, :], o, start=False, stop=False, skip_group_check=True)
                    pe.matmul(psRank[:, 0:J * NBK], count_rest[:, :], o, start=False, stop=False, skip_group_check=True)
                    for j in range(1, J):
                        m = pe.matmul(rank4[:, 0:j, :], ones_b[:, :], o[:, j:j + 1, :].to_broadcast([P, j, NBK]),
                                      start=False, stop=False, skip_group_check=True)
                    m.then_inc(counted, 1)
                if isinstance(s, int) and s in (0, G1):
                    c = 0 if s == 0 else 1
                    if c:
                        pe.wait_ge(slot_ready, s)
                    pe.matmul(rank4, ones_f[0:1, :], start_f[0:1, c:c + 1, :].to_broadcast([1, J, NBK]),
                              start=True, stop=False, skip_group_check=True)
                    if c:
                        pe.matmul(bank[7][0:2, 0:2], ones_b[:, 0:2], ones_b[:, 0:2], start=True, stop=True).then_inc(counted, 1)
                if have:
                    pe.wait_ge(hot_ready, s + 1)
                    o = hot[:, h, :, :]
                    m = pe.matmul(psRank[:, 0:J * NBK], count_own[:, :], o, start=False, stop=False, skip_group_check=True)
                    for j in range(J - 1):
                        m = pe.matmul(rank4[:, j + 1:J, :], ones_b[:, :], o[:, j:j + 1, :].to_broadcast([P, J - 1 - j, NBK]),
                                      start=False, stop=False, skip_group_check=True)
                    m.then_inc(rank_made, 1)
                    pe.wait_ge(ed_in[u], (i + 1) * 16)
                    for a in range(2):
                        m = pe.transpose(psT[:, a * P:a * P + P], ed[:, u, a * P:a * P + P], ident[:, :])
                    m.then_inc(edT_made, 1)
                    pe.wait_ge(rel_in[u // 2], (i + 1) * 16)
                    late(pe, onehot_ready, s)
                    pe.matmul(psRel[:, :], ones_b[0:1, :], rel_row[0:1, u // 2, h * GE:h * GE + GE],
                              start=True, stop=True).then_inc(rel_spread, 1)
                if have_prev:
                    pe.wait_ge(h1_ready, s)
                    late(pe, msg_ready, s - 1)
                    o = psH2[:, 0:J * D]
                    pe.matmul(o, ones_b[0:3, :], b2p[:, :], start=True, stop=False)
                    for a in range(2):
                        m = pe.matmul(o[:, a * P:a * P + P], h1[:, h1_, a * P:a * P + P], W2d[:, :], start=False, stop=(a == 1))
                    m.then_inc(h2_made, 1)
                    pe.wait_ge(onehot_ready, s)
                    pe.wait_ge(win_in[(u - 1) % UNROLL], (i + 1) * 16 if u else i * 16)
                    late(pe, x_ready, s - 1)
                    for j in range(J):
                        m = pe.matmul(psX[:, j * D:j * D + D], onehot[:, h1_, j:GE:J],
                                      win[:, (u - 1) % UNROLL, :], start=True, stop=True)
                    m.then_inc(x_made, 1)
                if have:
                    pe.wait_ge(edT_ready, s + 1)
                    late(pe, h1_ready, s)
                    pe.matmul(psH1[:, 0:2 * P], W1d[:, :], edT[:, h, :], start=True, stop=True).then_inc(h1_made, 1)

            def block(b, u, use):
                pe.wait_ge(pick_ready, b + 1)
                late(pe, sum_kept, b - 1)
                for k in range(CAP[0]):
                    m = pe.matmul(psSums[u % 2][:, 0:ACC], pick[:, u % 2, k, :], back0[:, u, k, 0:ACC],
                                  start=(k == 0), stop=(k == CAP[0] - 1))
                m.then_inc(sum_made, 1)

            def tail(i, r):
                pe.wait_ge(sums_ready, i + (r - 1)) if not (isinstance(i, int) and i + r - 1 <= 0) else None
                if isinstance(i, int) and i == 0:
                    pe.wait_ge(sum_kept, NB)
                for k in range(FB):
                    h = (r * FB + k) % 2
                    pe.wait_ge(pick_ready, i * FB + (NB + r * FB + k + 1))
                    for c in range(CAP[1]):
                        m = pe.matmul(psSums[r][:, k * ACC:(k + 1) * ACC], pick[:, h, c, :], back1[:, k, c, 0:ACC],
                                      start=(c == 0), stop=(c == CAP[1] - 1))
                    m.then_inc(sum_made, 1)

            with pe.If(general < 1):
                run_steps(pe, step, block, 1)
                tail(0, 0)
                tail(0, 1)
                with pe.Fori(1, NF // 2) as i:
                    tail(i * 2, 0)
                    tail(i * 2, 1)
            with pe.Else():
                with pe.Fori(0, GN) as i:
                    pe.wait_ge(g_in, i * 48 + 48)
                    pe.wait_ge(g_dve, i * 9 + 2)
                    pe.sem_inc(pe_event, 1)
                    pe.transpose(psT[0:D, 0:GP], g_ed[0:GP, :], ident[0:GP, 0:GP])
                    pe.transpose(psRel[0:GP, 0:GP], g_srcb[0:GP, 0:GP], ident[0:GP, 0:GP]).then_inc(g_pe, 1)
                    pe.wait_ge(g_act, i * 3 + 1)
                    pe.sem_inc(pe_event, 1)
                    pe.matmul(psH1[0:D, 0:GP], W1d[0:D, 0:D], g_edT[:, 0:GP], start=True, stop=True).then_inc(g_pe, 1)
                    pe.wait_ge(g_act, i * 3 + 2)
                    pe.matmul(psH2[0:GP, 0:D], ones_b[0:3, 0:GP], b2p[:, 0:D], start=True, stop=False)
                    pe.matmul(psH2[0:GP, 0:D], g_h1[:, 0:GP], W2d[0:D, 0:D], start=False, stop=True).then_inc(g_pe, 1)
                    pe.wait_ge(g_dve, i * 9 + 8)
                    pe.matmul(psSum[0:GP, 0:ACC], g_same[0:GP, 0:GP], g_msg[0:GP, :], start=True, stop=True).then_inc(g_pe, 1)

        @block_.scalar
        def _(act):
            act.dma_start(b1c[0:D, :], b1.rearrange("(p a) -> p a", a=1)).then_inc(weights_in, 16)
            act.dma_start(b1c[D:P, :], b1.rearrange("(p a) -> p a", a=1)).then_inc(weights_in, 16)
            act.dma_start(coef_b[:, :], coef.rearrange("f a -> a f").to_broadcast([P, D])).then_inc(weights_in, 16)
            act.dma_start(b2f[:, :].rearrange("p (j f) -> p j f", f=D),
                          b2.rearrange("(a c f) -> a c f", a=1, c=1).to_broadcast([3, J, D])).then_inc(weights_in, 16)
            act.wait_ge(consts, 2)
            for W, tile in ((W1, W1d), (W2, W2d)):
                act.dma_start(tile[0:D, 0:D], W).then_inc(matrices_in, 16)
                act.dma_start(tile[D:P, D:P], W).then_inc(matrices_in, 16)
            act.wait_ge(dst_in, 64)
            act.wait_ge(iotas, 3 + PASSES)
            for c in range(PASSES):
                rest = CAP[c] - FULL[c]
                act.dma_start(
                    rows_dram[PART[c]:PART[c] + NB * CAP[c] * P, :].rearrange("(b r) f -> b (r f)", b=NB)[:, FULL[c] * P * ROW:].rearrange("b (p f) -> p b f", p=P),
                    zero[:, 0:rest * ROW].rearrange("p (a f) -> p a f", a=1).to_broadcast([P, NB, rest * ROW])).then_inc(zeroed, 16)
                r0 = PART[c] + (NB - 1) * CAP[c] * P
                act.dma_start(rows_dram[r0:r0 + FULL[c] * P, :].rearrange("(p k) f -> p (k f)", p=P),
                              zero[:, 0:FULL[c] * ROW]).then_inc(zeroed, 16)
            act.wait_ge(src_in, 48)
            nc.scalar.copy(src4f[:, :, :], src4[:, :, :]).then_inc(src_float, 1)
            act.wait_ge(dst_in, 64)
            nc.scalar.copy(dst4f[:, :, :], dst4[:, :, :]).then_inc(dst_float, 1)
            for t in range(GT):
                n = min(P, T // J - t * P)
                act.wait_ge(src_turned, t + 1)
                nc.scalar.copy(srcT[:, t * P * J:t * P * J + n * J].rearrange("p (g j) -> p j g", j=J),
                               bank[t][:, :].rearrange("p (j g) -> p j g", j=J)[:, :, 0:n]).then_inc(src_back, 1)
            act.wait_ge(flag_ready, 1)
            general = act.value_load(flag_i[0:1, 0:1], min_val=0, max_val=1)

            def step(s, u, i):
                h = u % 2
                if real(s):
                    act.wait_ge(edT_made, s + 1)
                    late(act, h1_made, s - 1)
                    nc.scalar.copy(edT[:, h, :], psT[:, 0:2 * P]).then_inc(edT_ready, 1)
                if real(s - 1):
                    act.wait_ge(x_made, s)
                    late(act, msg_ready, s - 2)
                    nc.scalar.copy(xg[:, 1 - h, :, :], psX[:, 0:J * D]).then_inc(x_ready, 1)
                if real(s - 2):
                    v = (u + 2) % UNROLL
                    act.wait_ge(score_ready, s - 1)
                    nc.scalar.copy(rows[:, v, :, LOW], low_f[:, bass.ds((s - 2) * J, J)])
                    nc.scalar.activation(rows[:, v, :, ATT], score[:, h, :], ACT.Exp).then_inc(att_ready, 1)
                if real(s):
                    act.wait_ge(h1_made, s + 1)
                    late(act, h2_made, s - 1)
                    nc.scalar.activation(h1[:, h, :], psH1[:, 0:2 * P], ACT.Tanh, bias=b1c[:, 0:1]).then_inc(h1_ready, 1)
                if real(s - 2):
                    act.wait_ge(att_ready, s - 1)
                    for j in range(J):
                        m = nc.scalar.mul(rows[:, v, j, 0:D], rows[:, v, j, 0:D], rows[:, v, j, ATT:ATT + 1])
                    m.then_inc(rows_ready, 1)

            def block(b, u, use):
                act.wait_ge(sum_made, b + 1)
                nc.scalar.copy(acc[:, bass.ds(b, 1), :], psSums[u % 2][:, 0:ACC]).then_inc(sum_kept, 1)

            with act.If(general < 1):
                act.wait_ge(weights_in, 16 * 4)
                run_steps(act, step, block, 2)
            with act.Else():
                act.wait_ge(weights_in, 16 * 4)
                with act.Fori(0, GN) as i:
                    act.wait_ge(g_pe, i * 4 + 1)
                    nc.scalar.copy(g_edT[:, 0:GP], psT[0:D, 0:GP]).then_inc(g_act, 1)
                    act.wait_ge(g_pe, i * 4 + 2)
                    nc.scalar.activation(g_h1[:, 0:GP], psH1[0:D, 0:GP], ACT.Tanh, bias=b1c[0:D, 0:1]).then_inc(g_act, 1)
                    act.wait_ge(g_dve, i * 9 + 7)
                    nc.scalar.activation(g_n[0:GP, 2:3], g_n[0:GP, 1:2], ACT.Exp).then_inc(g_act, 1)
            for n in range(NF):
                q = n % 2
                act.wait_ge(y_centred, n + 1)
                nc.scalar.activation(sq[:, q, :, :], y[:, q, :, :], ACT.Square).then_inc(y_squared, 1)
                act.wait_ge(var_ready, n + 1)
                nc.scalar.activation(var[:, q, :, :], var[:, q, :, :], ACT.Sqrt).then_inc(std_ready, 1)
                act.wait_ge(y_ready, n + 1)
                b = n * FB
                if n < NF - 1:
                    act.dma_start(out[b * P:(b + FB) * P, :].rearrange("(b p) f -> p b f", p=P), y[:, q, :, :]).then_inc(out_done[q], 16)
                else:
                    act.dma_start(out[b * P:(b + FB - 1) * P, :].rearrange("(b p) f -> p b f", p=P), y[:, q, 0:FB - 1, :]).then_inc(out_done[q], 16)
                    act.dma_start(out[(NB - 1) * P:N, :], y[0:NL, q, FB - 1, :]).then_inc(out_done[q], 16)
            act.wait_ge(out_done[0], 16 * (NF // 2))
            act.wait_ge(out_done[1], 16 * (NF // 2 + 1))

        @block_.vector
        def _(dve):
            at = [0]

            def link(ins):
                at[0] += 1
                ins.then_inc(dve_step, 1)
                dve.wait_ge(dve_step, at[0])

            nc.vector.memset(src4[:, :, :], NB * P).then_inc(memset_done, 1)
            nc.vector.memset(dst4[:, :, :], 0).then_inc(memset_done, 1)
            nc.vector.memset(W1d[:, :], 0.0)
            nc.vector.memset(W2d[:, :], 0.0)
            nc.vector.memset(ones_f[:, :], 1.0)
            nc.vector.memset(ones_b[:, :], 1.0)
            dve.wait_ge(iotas, 2 + PASSES)
            nc.vector.tensor_copy(iota_n[:, :], iota_i[:, :])
            link(nc.vector.tensor_copy(part[:, :], part_i[:, :]))
            nc.vector.tensor_scalar(ident[:, :], iota_n[:, :], part[:, 0:1], None, ALU.is_equal).then_inc(consts, 1)
            nc.vector.tensor_copy(iota_b[:, :], iota_n[:, :])
            nc.vector.tensor_scalar(earlier[:, :], iota_n[:, :], part[:, 0:1], None, ALU.is_gt)
            nc.vector.tensor_scalar(later_f[:, :], iota_n[:, :], part[:, 0:1], None, ALU.is_lt)
            nc.vector.tensor_scalar(count_rest[:, :], iota_n[:, :], part[:, 0:1], None, ALU.is_le)
            nc.vector.tensor_scalar(digit_i[:, 0:1], part_i[:, :], 3, None, ALU.logical_shift_right)
            nc.vector.tensor_scalar(digit_i[:, 1:2], part_i[:, :], NHI - 1, None, ALU.bitwise_and)
            for c in range(PASSES):
                nc.vector.tensor_scalar(start_f[0:1, c, :], start_i[0:1, c, :], -BIG, None, ALU.add)
            link(nc.vector.memset(maskt[:, :], 0.0))
            nc.vector.memset(start_f[0:1, 0, NB:NBK], float(DUMP) - BIG)
            nc.vector.memset(start_f[0:1, 1, NB:NBK], float(DUMP) - BIG)
            nc.vector.scalar_tensor_tensor(out=count_own[:, :], in0=ident[:, :], scalar=BIG, in1=earlier[:, :], op0=ALU.mult, op1=ALU.add)
            nc.vector.tensor_scalar(drop_own[:, :], ident[:, :], -BIG, None, ALU.mult)
            link(nc.vector.tensor_copy(digit[:, :], digit_i[:, :]))
            nc.vector.tensor_scalar(maskt[:, :], iota_n[:, 0:NLO], digit[:, 0:1], None, ALU.is_equal)
            nc.vector.tensor_scalar(maskk[:, :], iota_n[:, 0:NHI], digit[:, 1:2], None, ALU.is_equal).then_inc(consts, 1)
            dve.wait_ge(weights_in, 16 * 4)
            link(nc.vector.tensor_copy(b2h[:, :], b2f[:, :]))
            link(nc.vector.tensor_scalar(b2s[:, :], b2h[:, :], ident[0:3, 0:1], None, ALU.mult))
            for k in (1, 2):
                link(nc.vector.tensor_tensor(b2f[:, :], b2f[:, :], b2h[:, :], ALU.subtract))
                link(nc.vector.tensor_copy(b2h[:, :], b2f[:, :]))
                link(nc.vector.tensor_scalar(b2r[:, :], b2h[:, :], ident[0:3, k:k + 1], None, ALU.mult))
                link(nc.vector.tensor_tensor(b2s[:, :], b2s[:, :], b2r[:, :], ALU.add))
            nc.vector.tensor_copy(b2p[:, :], b2s[:, :]).then_inc(b2_ready, 1)
            dve.wait_ge(src_back, GT)
            nc.vector.tensor_scalar(blkT[:, :], srcT[:, :], 7, None, ALU.logical_shift_right)
            link(nc.vector.tensor_scalar(srcT[:, :], srcT[:, :], P - 1, None, ALU.bitwise_and))
            nc.vector.tensor_copy(block_b[:, :], blkT[:, :])
            link(nc.vector.tensor_copy(low_f[:, :], srcT[:, :]))
            link(nc.vector.tensor_scalar(srcT[:, :], blkT[:, :], 4, None, ALU.logical_shift_right))
            link(nc.vector.tensor_copy(digit_b[:, 0, :], srcT[:, :]))
            link(nc.vector.tensor_scalar(blkT[:, :], blkT[:, :], NLO - 1, None, ALU.bitwise_and))
            link(nc.vector.tensor_copy(digit_b[:, 1, :], blkT[:, :]))
            for k in range(NHI):
                nc.vector.tensor_scalar(hot_hi[:, :, k], digit_b[:, 0, :], float(k), None, ALU.is_equal)
            for k in range(NLO):
                m = nc.vector.tensor_scalar(hot_lo[:, k, :], digit_b[:, 1, :], float(k), None, ALU.is_equal)
            m.then_inc(digits, 1)
            dve.wait_ge(dst_float, 1)
            link(nc.vector.tensor_scalar(base_f[:, :], dst4f[:, :, 0], float(XB), None, ALU.min))
            nc.vector.tensor_copy(base_i[:, :], base_f[:, :]).then_inc(dst_rel, 1)
            for t in range(GT):
                m = nc.vector.tensor_scalar(dst4f[:, t, :], dst4f[:, t, :], base_f[:, t:t + 1], None, ALU.subtract)
            link(m)
            nc.vector.tensor_copy(rel[:, :, :], dst4f[:, :, :]).then_inc(dst_rel, 1)
            nc.vector.tensor_reduce(viol[:, 4:5], dst4f[:, :, :], AX.XY, ALU.max)
            link(nc.vector.tensor_reduce(viol[:, 5:6], dst4f[:, :, :], AX.XY, ALU.min))
            nc.vector.tensor_scalar(viol[:, 4:5], viol[:, 4:5], float(P - 1), None, ALU.is_gt)
            nc.vector.tensor_scalar(viol[:, 5:6], viol[:, 5:6], 0.0, None, ALU.is_lt)
            dve.wait_ge(hist_made, 1)
            link(nc.vector.tensor_tensor(hist_m[:, :, :, :].rearrange("p c l t -> p (c l) t"), bank[4][:, :].rearrange("p (l t) -> p l t", t=NLO),
                                         maskt[:, :].rearrange("p (a t) -> p a t", a=1).to_broadcast([P, PASSES * NLO, NLO]), ALU.mult))
            link(nc.vector.tensor_reduce(hist_r[:, :, :], hist_m[:, :, :, :], AX.X, ALU.add))
            for c in range(PASSES):
                m = nc.vector.tensor_tensor(hist_x[:, c, :, :], hist_r[:, c:c + 1, :].to_broadcast([P, NHI, NLO]),
                                            maskk[:, :].rearrange("p (k a) -> p k a", a=1).to_broadcast([P, NHI, NLO]), ALU.mult)
            m.then_inc(hist_ready, 1)
            dve.wait_ge(counts_made, 1)
            counts = bank[5][:, 0:PASSES * NHI * NLO].rearrange("p (c b) -> p c b", c=PASSES)[:, :, 0:NB]
            nc.vector.tensor_reduce(viol[:, 0:2], counts, AX.X, ALU.max)
            link(nc.vector.tensor_reduce(viol[:, 2:4], counts[:, :, 0:NB - 1], AX.X, ALU.min))
            nc.vector.memset(viol[:, 6:8], 0.0)
            for c in range(PASSES):
                nc.vector.tensor_scalar(viol[:, c:c + 1], viol[:, c:c + 1], float(CAP[c] * P), None, ALU.is_gt)
                m = nc.vector.tensor_scalar(viol[:, 2 + c:3 + c], viol[:, 2 + c:3 + c], float(FULL[c] * P), None, ALU.is_lt)
            m.then_inc(viol_ready, 1)
            dve.wait_ge(viol_made, 1)
            link(nc.vector.tensor_reduce(viol[:, 0:1], bank[6][:, 0:8], AX.X, ALU.max))
            nc.vector.tensor_scalar(flag_i[0:1, 0:1], viol[0:1, 0:1], 0.0, None, ALU.is_gt).then_inc(flag_ready, 1)
            dve.wait_ge(flag_ready, 1)
            general = dve.value_load(flag_i[0:1, 0:1], min_val=0, max_val=1)
            coef_j = coef_b[:, :].rearrange("p (a f) -> p a f", a=1).to_broadcast([P, J, D])
            iota_j = iota_b[:, 0:NBK].rearrange("p (a b) -> p a b", a=1).to_broadcast([P, J, NBK])

            def make_hot(s, u):
                late(dve, counted, s - 1)
                nc.vector.tensor_tensor(hot[:, u % 2, :, :], iota_j,
                                        block_b[:, bass.ds(s * J, J)].rearrange("p (j a) -> p j a", a=1).to_broadcast([P, J, NBK]),
                                        ALU.is_equal).then_inc(hot_ready, 1)

            def step(s, u, i):
                h = u % 2
                if isinstance(s, int) and s == 0:
                    make_hot(0, 0)
                if real(s):
                    dve.wait_ge(rank_made, s + 1)
                    late(dve, scattered[u], i * (16 * J))
                    nc.vector.tensor_reduce(slot[:, u, :], psRank[:, 0:J * NBK].rearrange("p (j b) -> p j b", j=J), AX.X, ALU.max).then_inc(slot_ready, 1)
                    dve.wait_ge(rel_spread, s + 1)
                    late(dve, x_made, s - 1)
                    nc.vector.tensor_scalar(onehot[:, h, :], psRel[:, :], part[:, 0:1], None, ALU.is_equal).then_inc(onehot_ready, 1)
                if real(s - 1):
                    v = (u - 1) % UNROLL
                    dve.wait_ge(h2_made, s)
                    dve.wait_ge(x_ready, s)
                    nc.vector.tensor_tensor(rows[:, v, :, 0:D], psH2[:, 0:J * D].rearrange("p (j f) -> p j f", j=J),
                                            xg[:, 1 - h, :, :], ALU.mult).then_inc(msg_ready, 1)
                if real(s + 1) and not (isinstance(s, int) and s + 1 == NG):
                    make_hot(s + 1, u + 1)
                if real(s - 1):
                    dve.wait_ge(msg_ready, s)
                    late(dve, score_ready, s - 1)
                    nc.vector.tensor_tensor(weighted[:, :, :], rows[:, v, :, 0:D], coef_j, ALU.mult).then_inc(weighted_ready, 1)
                    dve.wait_ge(weighted_ready, s)
                    late(dve, att_ready, s - 2)
                    nc.vector.tensor_reduce(score[:, 1 - h, :], weighted[:, :, :], AX.X, ALU.add).then_inc(score_ready, 1)

            def picks(q, cap, low):
                return nc.vector.tensor_tensor(pick[:, q, 0:cap, :], iota_n[:, :].rearrange("p (a n) -> p a n", a=1).to_broadcast([P, cap, P]),
                                               low.to_broadcast([P, cap, P]), ALU.is_equal)

            def block(b, u, use):
                dve.wait_ge(back0_in[u], use * 16 + 16)
                late(dve, sum_made, b - 1)
                picks(u % 2, CAP[0], back0[:, u, :, LOW:LOW + 1]).then_inc(pick_ready, 1)

            def tail(i, r):
                n = i + r
                for k in range(FB):
                    h = (r * FB + k) % 2
                    dve.wait_ge(back1_in[k], (n + 1) * 16)
                    dve.wait_ge(sum_made, i * FB + (NB + r * FB + k - 1))
                    picks(h, CAP[1], back1[:, k, :, LOW:LOW + 1]).then_inc(pick_ready, 1)
                    if k == 3:
                        finish_second(i, r)
                    if k == 5:
                        finish_third(i, r)
                dve.wait_ge(sum_made, i * FB + (NB + r * FB + FB))
                b = i * FB + r * FB
                nc.vector.tensor_tensor(acc[:, bass.ds(b, FB), :], acc[:, bass.ds(b, FB), :],
                                        psSums[r][:, 0:FB * ACC].rearrange("p (b f) -> p b f", b=FB), ALU.add).then_inc(sums_ready, 1)
                finish_first(i, r)

            def finish_first(i, r):
                n = i + r
                b = n * FB
                dve.wait_ge(sums_ready, n + 1)
                late(dve, y_scaled, n - 1)
                nc.vector.tensor_scalar(fix[:, r, :, :], acc[:, bass.ds(b, FB), D:D + 1], 0.0, None, ALU.is_le).then_inc(fixed, 1)
                dve.wait_ge(fixed, n + 1)
                nc.vector.tensor_tensor(fix[:, r, :, :], acc[:, bass.ds(b, FB), D:D + 1], fix[:, r, :, :], ALU.add).then_inc(den_added, 1)
                dve.wait_ge(den_added, n + 1)
                nc.vector.reciprocal(den[:, r, :, :], fix[:, r, :, :]).then_inc(den_ready, 1)

            def finish_second(i, r):
                q = 1 - r
                n = i + (r - 1)
                if isinstance(n, int) and n < 0:
                    return
                dve.wait_ge(y_added, n + 1)
                nc.vector.tensor_reduce(mean[:, q, :, 0], y[:, q, :, :], AX.X, ALU.add).then_inc(y_summed, 1)
                dve.wait_ge(y_summed, n + 1)
                nc.vector.tensor_scalar(mean[:, q, :, :], mean[:, q, :, :], 1.0 / D, None, ALU.mult).then_inc(mean_ready, 1)
                dve.wait_ge(mean_ready, n + 1)
                nc.vector.tensor_tensor(y[:, q, :, :], y[:, q, :, :], mean[:, q, :, :].to_broadcast([P, FB, D]), ALU.subtract).then_inc(y_centred, 1)

            def finish_third(i, r):
                q = 1 - r
                n = i + (r - 1)
                if isinstance(n, int) and n < 0:
                    return
                dve.wait_ge(y_squared, n + 1)
                nc.vector.tensor_reduce(var[:, q, :, 0], sq[:, q, :, :], AX.X, ALU.add).then_inc(sq_summed, 1)
                dve.wait_ge(sq_summed, n + 1)
                nc.vector.tensor_scalar(var[:, q, :, :], var[:, q, :, :], 1.0 / D, 1e-5, ALU.mult, ALU.add).then_inc(var_ready, 1)
                dve.wait_ge(std_ready, n + 1)
                nc.vector.reciprocal(var[:, q, :, :], var[:, q, :, :]).then_inc(rstd_ready, 1)
                dve.wait_ge(rstd_ready, n + 1)
                nc.vector.tensor_tensor(y[:, q, :, :], y[:, q, :, :], var[:, q, :, :].to_broadcast([P, FB, D]), ALU.mult).then_inc(y_ready, 1)

            with dve.If(general < 1):
                nc.vector.memset(xres[:, NB - 1, :], 0.0).then_inc(xres_free, 1)
                run_steps(dve, step, block, 0)
                dve.wait_ge(sum_kept, NB)
                tail(0, 0)
                tail(0, 1)
                with dve.Fori(1, NF // 2) as i:
                    tail(i * 2, 0)
                    tail(i * 2, 1)
            with dve.Else():
                link2 = nc.vector.memset(shared[:, 0:NB * (ACC + D)], 0.0)
                link2.then_inc(memset_done, 1)
                dve.wait_ge(memset_done, 3)
                with dve.Fori(0, GN) as i:
                    dve.wait_ge(g_in, i * 48 + 48)
                    nc.vector.tensor_copy(g_srcf[0:GP, :], g_src[0:GP, :]).then_inc(g_dve, 1)
                    dve.wait_ge(g_dve, i * 9 + 1)
                    nc.vector.tensor_scalar(g_srcb[0:GP, :], iota_n[0:GP, :], 0.0, g_srcf[0:GP, 0:1], ALU.mult, ALU.add).then_inc(g_dve, 1)
                    dve.wait_ge(g_pe, i * 4 + 1)
                    nc.vector.tensor_scalar(g_same[0:GP, 0:GP], psRel[0:GP, 0:GP], g_srcf[0:GP, 0:1], None, ALU.is_equal).then_inc(g_dve, 1)
                    dve.wait_ge(g_dve, i * 9 + 3)
                    nc.vector.tensor_tensor(g_prev[0:GP, 0:GP], g_same[0:GP, 0:GP], later_f[0:GP, 0:GP], ALU.mult).then_inc(g_dve, 1)
                    dve.wait_ge(g_pe, i * 4 + 3)
                    dve.wait_ge(g_gathered, i * 32 + 32)
                    nc.vector.tensor_tensor(g_msg[0:GP, 0:D], psH2[0:GP, 0:D], g_x[0:GP, :], ALU.mult).then_inc(g_dve, 1)
                    dve.wait_ge(g_dve, i * 9 + 5)
                    nc.vector.tensor_tensor(g_t[0:GP, :], g_msg[0:GP, 0:D], coef_b[0:GP, :], ALU.mult).then_inc(g_dve, 1)
                    dve.wait_ge(g_dve, i * 9 + 6)
                    nc.vector.tensor_reduce(g_n[0:GP, 1:2], g_t[0:GP, :], AX.X, ALU.add).then_inc(g_dve, 1)
                    nc.vector.tensor_reduce(g_n[0:GP, 0:1], g_prev[0:GP, 0:GP], AX.X, ALU.max)
                    dve.wait_ge(g_act, i * 3 + 3)
                    nc.vector.tensor_copy(g_msg[0:GP, D:D + 1], g_n[0:GP, 2:3])
                    nc.vector.tensor_scalar(g_msg[0:GP, 0:D], g_msg[0:GP, 0:D], g_n[0:GP, 2:3], None, ALU.mult).then_inc(g_dve, 1)
                    dve.wait_ge(g_dve, i * 9 + 8)
                    nc.vector.scalar_tensor_tensor(out=g_n[0:GP, 3:4], in0=part[0:GP, :], scalar=float(NB * P), in1=g_srcf[0:GP, :], op0=ALU.add, op1=ALU.subtract)
                    dve.wait_ge(g_pe, i * 4 + 4)
                    nc.vector.tensor_tensor(g_msg[0:GP, :], psSum[0:GP, 0:ACC], g_sum[0:GP, :], ALU.add)
                    dve.drain()
                    nc.vector.scalar_tensor_tensor(out=g_to[0:GP, :], in0=g_n[0:GP, 3:4], scalar=g_n[0:GP, 0:1], in1=g_srcf[0:GP, :], op0=ALU.mult, op1=ALU.add).then_inc(g_dve, 1)
                dve.wait_ge(g_done, GN * 16)
                nc.vector.memset(xres[:, NB - 1, :], 0.0).then_inc(xres_free, 1)
                dve.wait_ge(g_back, 16)
                nc.vector.engine_nop().then_inc(sums_ready, NF)
                for i in range(0, NF, 2):
                    for r in range(2):
                        finish_first(i, r)
                        finish_second(i, r)
                        finish_third(i, r)
            finish_second(NF, 0)
            finish_third(NF, 0)


_INS = ["x", "src", "dst", "edge_attr_64", "L0_gnn_W1", "L0_gnn_b1", "L0_gnn_W2", "L0_gnn_b2", "L0_gnn_linear_coef"]


def kernel(**inputs):
    import numpy as _np
    import concourse.bacc as _bacc
    from concourse import mybir as _mybir
    from concourse.bass_utils import run_bass_kernel_spmd as _run

    nc = _bacc.Bacc("TRN2", target_bir_lowering=False, num_devices=1)
    arrays, args = {}, []
    for name in _INS:
        a = _np.ascontiguousarray(inputs[name])
        arrays[f"in_{name}"] = a
        args.append(nc.dram_tensor(f"in_{name}", a.shape, _mybir.dt.from_np(a.dtype), kind="ExternalInput").ap())
    shape = inputs["x"].shape
    args.append(nc.dram_tensor("out", shape, _mybir.dt.float32, kind="ExternalOutput").ap())
    node_sums_kernel(nc, *args)
    r = _run(nc, [arrays], core_ids=[0])
    return r.results[0]["out"]
```

```python
from contextlib import ExitStack

import concourse.bass as bass
from concourse import mybir

ALU = mybir.AluOpType
ACT = mybir.ActivationFunctionType
AX = mybir.AxisListType
F32 = mybir.dt.float32
BF16 = mybir.dt.bfloat16
I32 = mybir.dt.int32
U32 = mybir.dt.uint32

P = 128
D = 64
J = 4
GE = P * J
ROW = 66
ATT, LOW = D, D + 1
ACC = D + 1
BIG = float(1 << 18)
UNROLL = 4
BODIES = (0, 26, 52, 78)
PARTS = len(BODIES)
CAP = (5, 5, 5, 4)
FULL = (448, 448, 448, 320)


def node_sums_kernel(nc, x, src, dst, edge, W1, b1, W2, b2, coef, out):
    N = x.shape[0]
    E = src.shape[0]
    NG = -(-E // GE)
    EL = E - (NG - 1) * GE
    PL = EL // J
    NB = -(-N // P)
    NL = N - (NB - 1) * P
    NBK = NB + 1
    STARTS = tuple(UNROLL * i for i in BODIES)
    T = -(-NG * J // 16) * 16
    GT = -(-NG // P)
    GREST = NG - 1 - (GT - 1) * P
    PART = tuple(NB * sum(CAP[:c]) * P for c in range(PARTS))
    DUMP = NB * sum(CAP) * P
    ROWS = DUMP + GE
    LAST_WINDOW = N - P
    XP, XC, XSLOTS = 125, 20, 8
    XN = N // (XP * XC)
    FIRST = 2
    assert XP * XC * XN == N and XN * XSLOTS >= 4 * 7
    NHI, NLO = 8, 16
    FB = 7
    NF = NB // FB
    assert NF * FB == NB and NF % 2 == 0
    TAIL = (PARTS - 1) * NB
    CLEARS = (3, BODIES[1] - 2) + tuple(BODIES[c] - BODIES[c - 1] - 4 for c in range(2, PARTS))
    DST_COLUMN = 2 * PARTS
    ZP = 64
    LAG = 2
    assert EL % J == 0 and NB <= NHI * NLO and ROWS < BIG and GREST >= 0
    assert UNROLL * J == 16 and T - NG * J < GE * J and NG % UNROLL == 3 and D * 2 == P
    assert len(set(CAP[:-1])) == 1 and NB % 2 == 0

    rows_dram = nc.dram_tensor("scattered_rows", [ROWS, ROW], F32).ap()
    rel_dram = nc.dram_tensor("relative_dst", [GT * P, GE], BF16).ap()
    parts_dram = nc.dram_tensor("x_in_parts", [N, 3 * D], BF16).ap()
    base_dram = nc.dram_tensor("window_bases", [1, GT * P], I32).ap()
    GP = 125
    GN = E // GP
    assert GN * GP == E
    sums_dram = nc.dram_tensor("general_sums", [NB * P + P, ACC], F32).ap()

    with ExitStack() as ctx:
        def sb(name, shape, dt=F32):
            return ctx.enter_context(nc.sbuf_tensor(name, shape, dt))

        def sem(name):
            return ctx.enter_context(nc.semaphore(name))

        bank = [ctx.enter_context(nc.psum_tensor(f"bank{b}", [P, 512], F32)) for b in range(8)]

        iota_i = sb("iota_i", [P, P], I32)
        part_i = sb("part_i", [P, 1], I32)
        digit_i = sb("digit_i", [P, 2], I32)
        iota_n = sb("iota_n", [P, P])
        part = sb("part", [P, 1])
        digit = sb("digit", [P, 2])
        iota_b = sb("iota_b", [P, P], BF16)
        ident = sb("ident", [P, P])
        ones_f = sb("ones_f", [P, P])
        ones_b = sb("ones_b", [P, P], BF16)
        earlier = sb("earlier", [P, P])
        count_own = sb("count_own", [P, P], BF16)
        count_rest = sb("count_rest", [P, P], BF16)
        drop_own = sb("drop_own", [P, P], BF16)
        later_f = sb("later_f", [P, P])
        W1d = sb("W1d", [P, P])
        W2d = sb("W2d", [P, P])
        b1c = sb("b1c", [P, 1])
        b2f = sb("b2f", [3, J * D])
        b2r = sb("b2r", [3, J * D])
        b2s = sb("b2s", [3, J * D])
        b2h = sb("b2h", [3, J * D], BF16)
        b2p = sb("b2p", [3, J * D], BF16)
        coef_b = sb("coef_b", [P, D])
        start_i = sb("start_i", [1, PARTS, NBK], I32)
        start_f = sb("start_f", [1, PARTS, NBK])
        zero = sb("zero", [ZP, max(FULL) * ROW // ZP])

        index_i = sb("index_i", [P, 2, GT, GE], I32)
        index_f = sb("index_f", [P, 2, GT, GE])
        src4, dst4 = index_i[:, 0, :, :], index_i[:, 1, :, :]
        src4f, dst4f = index_f[:, 0, :, :], index_f[:, 1, :, :]
        base_f = sb("base_f", [P, GT])
        minus_base = sb("minus_base", [P, GT])
        minus_last = sb("minus_last", [P, 1])
        eps = sb("eps", [P, 1])
        base_i = sb("base_i", [P, GT], I32)
        rel = sb("rel", [P, GT, GE], BF16)
        srcT = sb("srcT", [P, T], I32)
        loT = sb("loT", [P, T], I32)
        hiT = sb("hiT", [P, T], I32)
        block_b = sb("block_b", [P, T], BF16)
        low_f = sb("low_f", [P, T])
        lo_b = sb("lo_b", [P, T], BF16)
        hist_m = sb("hist_m", [P, PARTS, NLO, NLO])
        hist_r = sb("hist_r", [P, PARTS, NLO])
        hist_x = sb("hist_x", [P, PARTS, NHI, NLO])
        maskt = sb("maskt", [P, NLO])
        maskk = sb("maskk", [P, NHI])
        viol = sb("viol", [P, 2 * PARTS + 2])
        flag_i = sb("flag_i", [1, 1], I32)
        base_row = sb("base_row", [1, GT * P], I32)

        shared = sb("shared", [P, (NHI + NLO) * T // 2])
        hot_hi = shared[:, 0:NHI * T // 2].bitcast(BF16).rearrange("p (t k) -> p t k", k=NHI)
        hot_lo = shared[:, NHI * T // 2:(NHI + NLO) * T // 2].bitcast(BF16).rearrange("p (k t) -> p k t", t=T)
        acc = shared[:, 0:NB * ACC].rearrange("p (b f) -> p b f", f=ACC)
        xres = shared[:, NB * ACC:NB * (ACC + D)].rearrange("p (b f) -> p b f", f=D)

        sumT = [t[0:ACC, 0:FB * P].bitcast(F32) for t in (hiT, loT)]
        work = sb("work", [P, XSLOTS * XN * D])
        xf = work[0:XP, :].rearrange("p (q r f) -> p q r f", q=XSLOTS, f=D)
        step_work = sb("step_work", [P, XSLOTS // 2 * XN * 3 * D])
        xparts = step_work[:, :].bitcast(BF16).rearrange("p (q r c f) -> p q r c f", q=XSLOTS, r=XN, c=3)
        edT = step_work[:, 0:2 * 2 * P].rearrange("p (h e) -> p h e", h=2)
        h1 = step_work[:, 4 * P:8 * P].rearrange("p (h e) -> p h e", h=2)
        xg = step_work[:, 8 * P:12 * P].rearrange("p (h j f) -> p h j f", h=2, j=J)
        rows = step_work[:, 12 * P:12 * P + UNROLL * J * ROW].rearrange("p (u j f) -> p u j f", u=UNROLL, j=J)

        ed = sb("ed", [P, UNROLL, J * D])
        win = sb("win", [P, UNROLL, 3, D], BF16)
        rel_row = sb("rel_row", [1, 2, 2 * GE], BF16)
        hot = sb("hot", [P, 2, J, NBK], BF16)
        slot = sb("slot", [P, UNROLL, J], U32)
        onehot = sb("onehot", [P, 2, GE], BF16)
        weighted = sb("weighted", [P, J, D])
        score = sb("score", [P, 2, J])
        table_i = index_i[:, :, :, :].bitcast(F32).rearrange("p a t e -> p (a t e)")
        table_f = index_f[:, :, :, :].rearrange("p a t e -> p (a t e)")
        B0 = 6 * CAP[0]
        back0 = table_i[:, 0:B0 * ROW].rearrange("p (u k f) -> p u k f", u=6, k=CAP[0])
        back1 = table_i[:, B0 * ROW:(B0 + FB * CAP[-1]) * ROW].rearrange("p (u k f) -> p u k f", u=FB, k=CAP[-1])
        pick0 = table_f[:, 0:B0 * P].rearrange("p (u k n) -> p u k n", u=6, k=CAP[0])
        pick1 = table_f[:, 0:FB * CAP[-1] * P].rearrange("p (u k n) -> p u k n", u=FB, k=CAP[-1])
        fix = sb("fix", [P, 2, FB, 1])
        den = sb("den", [P, 2, FB, 1])
        y = work[:, 0:2 * FB * D].rearrange("p (q k f) -> p q k f", q=2, f=D)
        mean = sb("mean", [P, 2, FB, 1])
        sq = work[:, 2 * FB * D:4 * FB * D].rearrange("p (q k f) -> p q k f", q=2, f=D)
        var = sb("var", [P, 2, FB, 1])
        g_ed = sb("g_ed", [P, D])
        g_src = sb("g_src", [P, 1], I32)
        g_dst = sb("g_dst", [P, 1], I32)
        g_srcf = sb("g_srcf", [P, 1])
        g_srcb = sb("g_srcb", [P, P])
        g_x = sb("g_x", [P, D])
        g_sum = sb("g_sum", [P, ACC])
        g_edT = sb("g_edT", [D, P])
        g_h1 = sb("g_h1", [D, P])
        g_same = sb("g_same", [P, P])
        g_prev = sb("g_prev", [P, P])
        g_n = sb("g_n", [P, 4])
        g_msg = sb("g_msg", [P, ACC])
        g_t = sb("g_t", [P, D])
        g_to = sb("g_to", [P, 1], U32)

        psT, psH1, psH2, psRel, psX, psRank = bank[:6]
        psSums = [bank[6], bank[7]]
        psTail = [[bank[0], bank[1]], [bank[2], bank[3]]]

        iotas = sem("iotas")
        consts = sem("consts")
        weights_in = sem("weights_in")
        matrices_in = sem("matrices_in")
        memset_done = sem("memset_done")
        src_in = sem("src_in")
        dst_in = sem("dst_in")
        src_float = sem("src_float")
        dst_float = sem("dst_float")
        dst_rel = sem("dst_rel")
        src_turned = sem("src_turned")
        src_back = sem("src_back")
        digits = sem("digits")
        low_ready = sem("low_ready")
        hist_made = sem("hist_made")
        hist_ready = sem("hist_ready")
        counts_made = sem("counts_made")
        viol_ready = sem("viol_ready")
        viol_made = sem("viol_made")
        flag_ready = sem("flag_ready")
        rel_out = sem("rel_out")
        rel_ready = sem("rel_ready")
        windows_checked = sem("windows_checked")
        x_in = [sem(f"x_in{q}") for q in range(XSLOTS)]
        x_high = sem("x_high")
        x_high0 = sem("x_high0")
        x_rest = sem("x_rest")
        x_middle = sem("x_middle")
        x_split = sem("x_split")
        x_stored = [sem(f"x_stored{q}") for q in range(XSLOTS)]
        base_in = sem("base_in")
        zeroed = [sem(f"zeroed{c}") for c in range(PARTS)]
        acc_cleared = sem("acc_cleared")
        dve_step = sem("dve_step")
        b2_ready = sem("b2_ready")
        ed_in = [sem(f"ed_in{u}") for u in range(UNROLL)]
        win_in = [sem(f"win_in{u}") for u in range(UNROLL)]
        rel_in = [sem(f"rel_in{q}") for q in range(2)]
        edT_made = sem("edT_made")
        edT_ready = sem("edT_ready")
        h1_made = sem("h1_made")
        h1_ready = sem("h1_ready")
        h2_made = sem("h2_made")
        rel_spread = sem("rel_spread")
        onehot_ready = sem("onehot_ready")
        x_made = sem("x_made")
        x_ready = sem("x_ready")
        hot_ready = sem("hot_ready")
        rank_made = sem("rank_made")
        slot_ready = sem("slot_ready")
        counted = sem("counted")
        msg_ready = sem("msg_ready")
        weighted_ready = sem("weighted_ready")
        att_ready = sem("att_ready")
        score_ready = sem("score_ready")
        rows_ready = sem("rows_ready")
        scattered = [sem(f"scattered{u}") for u in range(UNROLL)]
        back0_in = [sem(f"back0_in{u}") for u in range(6)]
        back1_in = [sem(f"back1_in{k}") for k in range(FB)]
        pick_ready = sem("pick_ready")
        sum_made = sem("sum_made")
        sum_kept = sem("sum_kept")
        pool_event = sem("pool_event")
        pe_event = sem("pe_event")
        g_zeroed = sem("g_zeroed")
        g_in = sem("g_in")
        g_gathered = sem("g_gathered")
        g_pe = sem("g_pe")
        g_act = sem("g_act")
        g_dve = sem("g_dve")
        g_done = sem("g_done")
        g_back = sem("g_back")
        xres_in = sem("xres_in")
        turned_kept = sem("turned_kept")
        turned_back = sem("turned_back")
        sums_ready = sem("sums_ready")
        fixed = sem("fixed")
        den_ready = sem("den_ready")
        y_scaled = sem("y_scaled")
        y_added = sem("y_added")
        y_summed = sem("y_summed")
        den_added = sem("den_added")
        mean_ready = sem("mean_ready")
        y_centred = sem("y_centred")
        y_squared = sem("y_squared")
        std_ready = sem("std_ready")
        rstd_ready = sem("rstd_ready")
        y_ready = sem("y_ready")
        out_done = [sem(f"out_done{q}") for q in range(2)]

        def late(eng, semaphore, value):
            if not (isinstance(value, int) and value <= 0):
                eng.wait_ge(semaphore, value)

        def real(s):
            return not isinstance(s, int) or 0 <= s < NG

        LAST = NG + 2
        PLACES = {0: (0, 0, 0, 0, 0, 0, 0, 0), 2: (0, 1, 0, 0, 0, 1, 0, 0), 4: (0, 1, 0, 1, 0, 1, 0, 1), 6: (1, 1, 0, 1, 1, 1, 0, 1)}

        def run_steps(eng, step, block, drain, clear=lambda c, b, n: None):
            uses, prev = [0] * 6, [None] * 6
            left_over = []

            def body(i, n, g, b, c, use, prev):
                left = list(range(n))

                def place(half):
                    if PLACES[n][half]:
                        j = left.pop(0)
                        block(g + j, b + j, j, use(j), prev(j), c)

                for u in range(UNROLL):
                    step(i * UNROLL + u, u, i, lambda: place(2 * u))
                    place(2 * u + 1)
                    if n == 0 and left_over:
                        drain(*left_over.pop(0))

            def still(i, n=0, g=0, b=0, c=0):
                body(i, n, g, b, c, lambda j: uses[j], lambda j: prev[j])
                for j in range(n):
                    uses[j] += 1
                    prev[j] = g + j

            still(0)
            still(1)
            with eng.Fori(2, BODIES[1]) as i:
                body(i, 0, 0, 0, 0, None, None)
                clear(1, i * 4 - 8, 4)
            clear(1, 4 * CLEARS[1], NB - 4 * CLEARS[1])
            for c in range(PARTS - 1):
                first = BODIES[c + 1]
                end = BODIES[c + 2] if c + 2 < PARTS else NG // UNROLL
                bodies = end - first - 2
                n = 4 if 4 * bodies + 2 >= NB else 6
                g0 = c * NB
                still(first)
                still(first + 1)
                still(first + 2, n, g0, 0, c)
                loop = bodies - 2
                i0 = first + 3
                with eng.Fori(i0, i0 + loop) as i:
                    body(i, n, i * n + (g0 + n - i0 * n), i * n + (n - i0 * n), c,
                         lambda j: i + (uses[j] - i0), lambda j: i * n + (g0 - i0 * n + j))
                    if c + 2 < PARTS:
                        clear(c + 2, i * 4 - i0 * 4, 4)
                if c + 2 < PARTS:
                    clear(c + 2, 4 * CLEARS[c + 2], NB - 4 * CLEARS[c + 2])
                for j in range(n):
                    uses[j] += loop
                    prev[j] = g0 + loop * n + j
                done = (loop + 1) * n
                still(end - 1, NB - done, g0 + done, done, c)
                left_over.extend((g0 + NB, NB, k) for k in range(LAG + 1))
            for s in range(NG // UNROLL * UNROLL, LAST):
                step(s, s % UNROLL, s // UNROLL, lambda: None)
                if left_over:
                    drain(*left_over.pop(0))

        def clear_first(eng, b, n):
            rest = (CAP[0] * P - FULL[0]) * ROW // ZP
            region = rows_dram[0:PART[1], :].rearrange("(b r) f -> b (r f)", b=NB)
            eng.dma_start(region[b:b + n, FULL[0] * ROW:].rearrange("b (p f) -> p b f", p=ZP),
                          zero[:, 0:rest].rearrange("p (a f) -> p a f", a=1).to_broadcast([ZP, n, rest])).then_inc(zeroed[0], 16)
            if b + n == NB:
                eng.dma_start(region[NB - 1, 0:FULL[0] * ROW].rearrange("(p f) -> p f", p=ZP), zero[:, 0:FULL[0] * ROW // ZP]).then_inc(zeroed[0], 16)

        block_ = ctx.enter_context(nc.Block())

        @block_.sync
        def _(sp):
            sp.wait_ge(memset_done, 2)
            for idx, tile, done in ((src, src4, src_in), (dst, dst4, dst_in)):
                whole = (GT - 1) * P * GE
                sp.dma_start(tile[:, 0:GT - 1, :], idx[0:whole].rearrange("(t p e) -> p t e", p=P, e=GE)).then_inc(done, 16)
                sp.dma_start(tile[0:GREST, GT - 1, :], idx[whole:(NG - 1) * GE].rearrange("(p e) -> p e", e=GE)).then_inc(done, 16)
                sp.dma_start(tile[GREST:GREST + 1, GT - 1, 0:EL], idx[(NG - 1) * GE:E].rearrange("(p e) -> p e", p=1)).then_inc(done, 16)
            sp.dma_start(dst4[GREST:GREST + 1, GT - 1, EL:GE], dst[E - (GE - EL):E].rearrange("(p e) -> p e", p=1)).then_inc(dst_in, 16)
            def load_chunk(n):
                r = n * XN * D
                q = n % XSLOTS
                sp.dma_start(work[0:XP, q * XN * D:(q + 1) * XN * D], x.rearrange("(p r) f -> p (r f)", p=XP)[:, r:r + XN * D]).then_inc(x_in[q], 16)

            for n in range(XSLOTS):
                load_chunk(n)
            sp.wait_ge(iotas, 3 + PARTS)
            clear_first(sp, 0, NB - CLEARS[0] * 14)
            for n in range(XC):
                sp.wait_ge(x_split, n + 1)
                r = n * XN * 3 * D
                sp.dma_start(parts_dram.rearrange("(p r) f -> p (r f)", p=XP)[:, r:r + XN * 3 * D],
                             xparts[0:XP, n % XSLOTS, :, :, :].rearrange("p r c f -> p (r c f)")).then_inc(x_stored[n % XSLOTS], 16)
                if n + XSLOTS < XC:
                    load_chunk(n + XSLOTS)
            sp.wait_ge(rel_out, 32)
            sp.dma_start(base_row[:, :], base_dram).then_inc(base_in, 16)
            sp.wait_ge(base_in, 16)

            def step(s, u, i, middle):
                if not real(s):
                    return
                middle()
                last = isinstance(s, int) and s == NG - 1
                np_ = PL if last else P
                if u == 0:
                    n = min(UNROLL, NG - s) if isinstance(s, int) else UNROLL
                    step.bases = nc.values_load_multi_w_load_instructions(
                        base_row[0:1, bass.ds(s, n)], engines=[mybir.EngineType.SP], min_val=0, max_val=LAST_WINDOW)[1]
                late(sp, edT_made, s - UNROLL + 1)
                sp.dma_start(ed[0:np_, u, :], edge[bass.ds(s * GE, np_ * J), :].rearrange("(p j) f -> p (j f)", j=J)).then_inc(ed_in[u], 16)
                if isinstance(s, int) and s == 0:
                    for q in range(XSLOTS):
                        sp.wait_ge(x_stored[q], 16 * len(range(q, XC, XSLOTS)))
                late(sp, x_made, s - UNROLL + 1)
                sp.dma_start(win[:, u, :, :].rearrange("p c f -> p (c f)"), parts_dram[bass.ds(step.bases[u], P), :]).then_inc(win_in[u], 16)
                if u % 2 == 1 or last:
                    e0, n = (s, 1) if last else (s - 1, 2)
                    sp.dma_start(rel_row[0:1, u // 2, 0:n * GE],
                                 rel_dram[bass.ds(e0, n), :].rearrange("g e -> (g e)").rearrange("(a e) -> a e", a=1)).then_inc(rel_in[u // 2], 16)

            sp.wait_ge(iotas, 4 + PARTS)
            for u in range(UNROLL):
                step(u, u, 0, lambda: None)
            sp.wait_ge(flag_ready, 1)
            general = sp.value_load(flag_i[0:1, 0:1], min_val=0, max_val=1)

            def later_steps(s, u, i, middle):
                if not (isinstance(s, int) and s < UNROLL):
                    step(s, u, i, middle)
                if isinstance(s, int) and STARTS[1] <= s < STARTS[-1]:
                    c = max(c for c in range(PARTS) if STARTS[c] <= s)
                    if s - STARTS[c] < NF // 2:
                        load_nodes((c - 1) * (NF // 2) + s - STARTS[c])

            def clear(c, b, n):
                C = CAP[c] * P
                region = rows_dram[bass.ds(b * C + PART[c], n * C), :].rearrange("(b r) f -> b (r f)", b=n)
                rest = (C - FULL[c]) * ROW // ZP
                sp.dma_start(region[:, FULL[c] * ROW:].rearrange("b (p f) -> p b f", p=ZP),
                             zero[:, 0:rest].rearrange("p (a f) -> p a f", a=1).to_broadcast([ZP, n, rest])).then_inc(zeroed[c], 16)
                if isinstance(b, int) and b + n == NB:
                    sp.dma_start(region[n - 1, 0:FULL[c] * ROW].rearrange("(p f) -> p f", p=ZP), zero[:, 0:FULL[c] * ROW // ZP]).then_inc(zeroed[c], 16)

            def block(g, b, u, use, prev, c):
                if isinstance(b, int) and b == 0:
                    for v in range(UNROLL):
                        sp.wait_ge(scattered[v], 16 * J * BODIES[c + 1])
                if prev is not None:
                    sp.wait_ge(sum_made, prev + 1)
                sp.dma_start(back0[:, u, :, :], rows_dram[bass.ds(b * (CAP[c] * P) + PART[c], CAP[c] * P), :].rearrange("(p k) f -> p k f", k=CAP[c])).then_inc(back0_in[u], 16)

            def load_nodes(n):
                b = n * FB
                sp.wait_ge(acc_cleared, 1)
                if n < NF - 1:
                    sp.dma_start(xres[:, b:b + FB, :], x[b * P:(b + FB) * P, :].rearrange("(b p) f -> p b f", p=P)).then_inc(xres_in, 16)
                else:
                    sp.dma_start(xres[:, b:b + FB - 1, :], x[b * P:(b + FB - 1) * P, :].rearrange("(b p) f -> p b f", p=P)).then_inc(xres_in, 16)
                    sp.dma_start(xres[0:NL, NB - 1, :], x[(NB - 1) * P:N, :]).then_inc(xres_in, 16)

            with sp.If(general < 1):
                run_steps(sp, later_steps, block, lambda g, b, k: None, clear)
                for u in range(UNROLL):
                    sp.wait_ge(scattered[u], 16 * J * len(range(u, NG, UNROLL)))
                C = CAP[-1] * P
                for k in range(FB):
                    sp.dma_start(back1[:, k, :, :], rows_dram[PART[-1] + k * C:PART[-1] + (k + 1) * C, :].rearrange("(p k) f -> p k f", p=P)).then_inc(back1_in[k], 16)
                with sp.Fori(1, NF) as i:
                    for k in range(FB):
                        sp.wait_ge(sum_made, i * FB + (TAIL + k + 1 - FB))
                        sp.dma_start(back1[:, k, :, :],
                                     rows_dram[bass.ds(i * (FB * C) + (PART[-1] + k * C), C), :].rearrange("(p k) f -> p k f", p=P)).then_inc(back1_in[k], 16)
            with sp.Else():
                for u in range(UNROLL):
                    sp.wait_ge(ed_in[u], 16)
                    sp.wait_ge(win_in[u], 16)
                    sp.wait_ge(rel_in[u // 2], 16)
                sp.wait_ge(zeroed[0], 16 * (CLEARS[0] + 2))
                sp.wait_ge(acc_cleared, 1)
                for c in range(2):
                    sp.dma_start(sums_dram[c * NB * P // 2:(c + 1) * NB * P // 2, :].rearrange("(p k) f -> p (k f)", p=P),
                                 acc[:, 0:NB // 2, :].rearrange("p b f -> p (b f)")).then_inc(g_zeroed, 16)
                sp.dma_start(sums_dram[NB * P:NB * P + P, :], acc[:, 0, :]).then_inc(g_zeroed, 16)
                with sp.Fori(0, GN) as i:
                    sp.wait_ge(g_done, i * 16)
                    sp.dma_start(g_ed[0:GP, :], edge[bass.ds(i * GP, GP), :]).then_inc(g_in, 16)
                    sp.dma_start(g_src[0:GP, :], src[bass.ds(i * GP, GP)].rearrange("(p a) -> p a", a=1)).then_inc(g_in, 16)
                    sp.dma_start(g_dst[0:GP, :], dst[bass.ds(i * GP, GP)].rearrange("(p a) -> p a", a=1)).then_inc(g_in, 16)
                sp.wait_ge(g_done, GN * 16)
                sp.dma_start(acc[:, :, :], sums_dram[0:NB * P, :].rearrange("(b p) f -> p b f", p=P)).then_inc(g_back, 16)
                for n in range(NF):
                    load_nodes(n)
        @block_.gpsimd
        def _(pool):
            nc.gpsimd.iota(iota_i[:, :], [[1, P]], base=0, channel_multiplier=0).then_inc(iotas, 1)
            nc.gpsimd.iota(part_i[:, :], [[1, 1]], base=0, channel_multiplier=1).then_inc(iotas, 1)
            for c in range(PARTS):
                nc.gpsimd.iota(start_i[0:1, c, :], [[CAP[c] * P, NBK]], base=PART[c], channel_multiplier=0).then_inc(iotas, 1)
            nc.gpsimd.memset(zero[:, :], 0.0).then_inc(iotas, 1)
            nc.gpsimd.memset(ed[:, :, :], 0.0).then_inc(iotas, 1)
            def split_low(n):
                q = n % XSLOTS
                pool.wait_ge(x_middle, n + 1)
                nc.gpsimd.tensor_tensor(xparts[0:XP, q, :, 2, :], xf[:, q, :, :], xparts[0:XP, q, :, 1, :], ALU.subtract).then_inc(x_split, 1)

            for n in range(XC):
                if n < FIRST:
                    pool.wait_ge(x_in[n], 16)
                    nc.gpsimd.tensor_copy(xparts[0:XP, n, :, 0, :], xf[:, n, :, :]).then_inc(x_high0, 1)
                    pool.wait_ge(x_high0, n + 1)
                else:
                    pool.wait_ge(x_high, n + 1 - FIRST)
                nc.gpsimd.tensor_tensor(xf[:, n % XSLOTS, :, :], xf[:, n % XSLOTS, :, :], xparts[0:XP, n % XSLOTS, :, 0, :], ALU.subtract).then_inc(x_rest, 1)
                if n > 0:
                    split_low(n - 1)
            split_low(XC - 1)
            pool.wait_ge(hist_made, 2)
            nc.gpsimd.memset(xres[:, NB - 1, :], 0.0)
            nc.gpsimd.memset(acc[:, :, :], 0.0).then_inc(acc_cleared, 1)
            pool.wait_ge(flag_ready, 1)
            general = pool.value_load(flag_i[0:1, 0:1], min_val=0, max_val=1)

            def step(s, u, i, middle):
                if isinstance(s, int) and s < 2:
                    return
                v = (u + 2) % UNROLL
                if isinstance(s, int) and s - 2 in STARTS:
                    pool.wait_ge(zeroed[STARTS.index(s - 2)], 16 * (CLEARS[STARTS.index(s - 2)] + 2))
                pool.wait_ge(rows_ready, s - 1)
                pool.sem_inc(pool_event, 1)
                for j in range(J):
                    nc.gpsimd.indirect_dma_start(
                        out=rows_dram[:, :], out_offset=bass.IndirectOffsetOnAxis(ap=slot[:, v, j:j + 1], axis=0),
                        in_=rows[:, v, j, :], in_offset=None).then_inc(scattered[v], 16)

            def finish_nodes_pool(pool):
                pool.wait_ge(xres_in, 16 * (NF + 1))
                for n in range(NF):
                    q = n % 2
                    b = n * FB
                    pool.wait_ge(den_ready, n + 1)
                    late(pool, out_done[q], 16 * (n // 2))
                    nc.gpsimd.tensor_tensor(y[:, q, :, :], acc[:, b:b + FB, 0:D], den[:, q, :, :].to_broadcast([P, FB, D]), ALU.mult).then_inc(y_scaled, 1)
                    pool.wait_ge(y_scaled, n + 1)
                    nc.gpsimd.tensor_tensor(y[:, q, :, :], y[:, q, :, :], xres[:, b:b + FB, :], ALU.add).then_inc(y_added, 1)
                    pool.wait_ge(mean_ready, n + 1)
                    nc.gpsimd.tensor_tensor(y[:, q, :, :], y[:, q, :, :], mean[:, q, :, :].to_broadcast([P, FB, D]), ALU.subtract).then_inc(y_centred, 1)

            with pool.If(general < 1):
                run_steps(pool, step, lambda *a: None, lambda g, b, k: None)
                finish_nodes_pool(pool)
            with pool.Else():
                pool.wait_ge(g_zeroed, 48)
                with pool.Fori(0, GN) as i:
                    pool.wait_ge(g_in, i * 48 + 48)
                    pool.sem_inc(pool_event, 1)
                    nc.gpsimd.indirect_dma_start(out=g_x[0:GP, :], out_offset=None, in_=x[:, :],
                                                 in_offset=bass.IndirectOffsetOnAxis(ap=g_dst[0:GP, 0:1].bitcast(U32), axis=0)).then_inc(g_gathered, 16)
                    nc.gpsimd.indirect_dma_start(out=g_sum[0:GP, :], out_offset=None, in_=sums_dram[:, :],
                                                 in_offset=bass.IndirectOffsetOnAxis(ap=g_src[0:GP, 0:1].bitcast(U32), axis=0)).then_inc(g_gathered, 16)
                    pool.wait_ge(g_dve, i * 9 + 9)
                    pool.sem_inc(pool_event, 1)
                    nc.gpsimd.indirect_dma_start(out=sums_dram[:, :], out_offset=bass.IndirectOffsetOnAxis(ap=g_to[0:GP, 0:1], axis=0),
                                                 in_=g_msg[0:GP, :], in_offset=None).then_inc(g_done, 16)
                pool.wait_ge(g_done, GN * 16)
                finish_nodes_pool(pool)

        @block_.tensor
        def _(pe):
            pe.wait_ge(src_float, 1)
            pe.wait_ge(consts, 1)
            for t in range(GT):
                n = min(P, T // J - t * P)
                for j in range(J):
                    m = pe.transpose(bank[t][:, j * P:j * P + n], src4f[0:n, t, j::J], ident[0:n, 0:n])
                m.then_inc(src_turned, 1)
            ends = [g * J for g in STARTS[1:]] + [T]
            for c in range(PARTS):
                t0, t1 = STARTS[c] * J, ends[c]
                pe.wait_ge(digits, c // 2 + 1)
                for t in range(t0, t1, 16):
                    m = pe.matmul(bank[6 + c // 2][:, c % 2 * 256:c % 2 * 256 + 256], hot_hi[:, t:t + 16, :].rearrange("p t k -> p (t k)"),
                                  hot_lo[:, :, t:t + 16], start=(t == t0), stop=(t + 16 >= t1))
                if c % 2 == 1:
                    m.then_inc(hist_made, 1)
            pe.wait_ge(hist_ready, 1)
            pe.matmul(bank[5][:, 0:PARTS * NHI * NLO], ones_f[:, :], hist_x[:, :, :, :], start=True, stop=True).then_inc(counts_made, 1)
            pe.wait_ge(viol_ready, 1)
            pe.wait_ge(windows_checked, 1)
            pe.matmul(bank[4][:, 0:2 * PARTS + 2], ones_f[:, :], viol[:, :], start=True, stop=True).then_inc(viol_made, 1)
            pe.wait_ge(matrices_in, 16 * 4)
            pe.wait_ge(b2_ready, 1)
            pe.wait_ge(consts, 2)
            pe.wait_ge(flag_ready, 1)
            general = pe.value_load(flag_i[0:1, 0:1], min_val=0, max_val=1)
            rank4 = psRank[:, 0:J * NBK].rearrange("p (j b) -> p j b", j=J)

            def step(s, u, i, middle):
                h = u % 2
                h1_, prev = 1 - h, s - 1
                have, have_prev = real(s), real(s - 1)
                if have_prev and not (isinstance(s, int) and s in STARTS):
                    pe.wait_ge(slot_ready, s)
                    o = hot[:, h1_, :, :]
                    pe.matmul(psRank[:, 0:J * NBK], drop_own[:, :], o, start=False, stop=False, skip_group_check=True)
                    pe.matmul(psRank[:, 0:J * NBK], count_rest[:, :], o, start=False, stop=False, skip_group_check=True)
                    for j in range(1, J):
                        m = pe.matmul(rank4[:, 0:j, :], ones_b[:, :], o[:, j:j + 1, :].to_broadcast([P, j, NBK]),
                                      start=False, stop=False, skip_group_check=True)
                    m.then_inc(counted, 1)
                if isinstance(s, int) and s in STARTS:
                    c = STARTS.index(s)
                    late(pe, slot_ready, s)
                    m = pe.matmul(rank4, ones_f[0:1, :], start_f[0:1, c:c + 1, :].to_broadcast([1, J, NBK]),
                                  start=True, stop=False, skip_group_check=True)
                    if s > 0:
                        m.then_inc(counted, 1)
                if have:
                    pe.wait_ge(hot_ready, s + 1)
                    o = hot[:, h, :, :]
                    m = pe.matmul(psRank[:, 0:J * NBK], count_own[:, :], o, start=False, stop=False, skip_group_check=True)
                    for j in range(J - 1):
                        m = pe.matmul(rank4[:, j + 1:J, :], ones_b[:, :], o[:, j:j + 1, :].to_broadcast([P, J - 1 - j, NBK]),
                                      start=False, stop=False, skip_group_check=True)
                    m.then_inc(rank_made, 1)
                    pe.wait_ge(ed_in[u], (i + 1) * 16)
                    for a in range(2):
                        m = pe.transpose(psT[:, a * P:a * P + P], ed[:, u, a * P:a * P + P], ident[:, :])
                    m.then_inc(edT_made, 1)
                    pe.wait_ge(rel_in[u // 2], (i + 1) * 16)
                    late(pe, onehot_ready, s)
                    pe.matmul(psRel[:, :], ones_b[0:1, :], rel_row[0:1, u // 2, h * GE:h * GE + GE],
                              start=True, stop=True).then_inc(rel_spread, 1)
                middle()
                if have_prev:
                    pe.wait_ge(h1_ready, s)
                    late(pe, msg_ready, s - 1)
                    o = psH2[:, 0:J * D]
                    pe.matmul(o, ones_b[0:3, :], b2p[:, :], start=True, stop=False)
                    for a in range(2):
                        m = pe.matmul(o[:, a * P:a * P + P], h1[:, h1_, a * P:a * P + P], W2d[:, :], start=False, stop=(a == 1))
                    m.then_inc(h2_made, 1)
                    pe.wait_ge(onehot_ready, s)
                    pe.wait_ge(win_in[(u - 1) % UNROLL], (i + 1) * 16 if u else i * 16)
                    late(pe, x_ready, s - 1)
                    for j in range(J):
                        for k in range(3):
                            m = pe.matmul(psX[:, j * D:j * D + D], onehot[:, h1_, j:GE:J],
                                          win[:, (u - 1) % UNROLL, k, :], start=(k == 0), stop=(k == 2))
                    m.then_inc(x_made, 1)
                if have:
                    pe.wait_ge(edT_ready, s + 1)
                    late(pe, h1_ready, s)
                    pe.matmul(psH1[:, 0:2 * P], W1d[:, :], edT[:, h, :], start=True, stop=True).then_inc(h1_made, 1)

            def sums(g, u, c):
                pe.wait_ge(pick_ready, g + 1)
                late(pe, sum_kept, g - 1)
                for k in range(CAP[c]):
                    m = pe.matmul(psSums[u % 2][:, 0:ACC], pick0[:, u, k, :], back0[:, u, k, 0:ACC],
                                  start=(k == 0), stop=(k == CAP[c] - 1))
                m.then_inc(sum_made, 1)

            slots = []

            def block(g, b, u, use, prev, c):
                slots.append(u)
                if not (isinstance(b, int) and b < LAG):
                    sums(g - LAG, slots[-1 - LAG], c)

            def drain(g, b, k):
                if k < LAG:
                    sums(g - LAG + k, slots[k - LAG], 0)

            def tail(i, r):
                n = i + r
                late(pe, turned_kept, n - 1)
                for k in range(FB):
                    if k == 2:
                        turn_back(i, r - 1)
                    pe.wait_ge(pick_ready, i * FB + (TAIL + r * FB + k + 1))
                    for c in range(CAP[-1]):
                        m = pe.matmul(psTail[r][k // 4][0:ACC, k % 4 * P:k % 4 * P + P], back1[:, k, c, 0:ACC], pick1[:, k, c, :],
                                      start=(c == 0), stop=(c == CAP[-1] - 1))
                    m.then_inc(sum_made, 1)

            def turn_back(i, r):
                if isinstance(i, int) and i + r < 0:
                    return
                n, q = i + r, r % 2
                pe.wait_ge(turned_kept, n + 1)
                late(pe, sums_ready, n - 1)
                for k in range(FB):
                    m = pe.transpose(psSums[q][:, k * ACC:(k + 1) * ACC], sumT[q][:, k * P:(k + 1) * P], ident[0:ACC, 0:ACC])
                m.then_inc(turned_back, 1)

            with pe.If(general < 1):
                run_steps(pe, step, block, drain)
                pe.wait_ge(sum_kept, TAIL)
                pe.wait_ge(rows_ready, NG)
                tail(0, 0)
                tail(0, 1)
                with pe.Fori(1, NF // 2) as i:
                    tail(i * 2, 0)
                    tail(i * 2, 1)
                turn_back(NF, -1)
            with pe.Else():
                with pe.Fori(0, GN) as i:
                    pe.wait_ge(g_in, i * 48 + 48)
                    pe.wait_ge(g_dve, i * 9 + 2)
                    pe.sem_inc(pe_event, 1)
                    pe.transpose(psT[0:D, 0:GP], g_ed[0:GP, :], ident[0:GP, 0:GP])
                    pe.transpose(psRel[0:GP, 0:GP], g_srcb[0:GP, 0:GP], ident[0:GP, 0:GP]).then_inc(g_pe, 1)
                    pe.wait_ge(g_act, i * 3 + 1)
                    pe.sem_inc(pe_event, 1)
                    pe.matmul(psH1[0:D, 0:GP], W1d[0:D, 0:D], g_edT[:, 0:GP], start=True, stop=True).then_inc(g_pe, 1)
                    pe.wait_ge(g_act, i * 3 + 2)
                    pe.matmul(psH2[0:GP, 0:D], ones_b[0:3, 0:GP], b2p[:, 0:D], start=True, stop=False)
                    pe.matmul(psH2[0:GP, 0:D], g_h1[:, 0:GP], W2d[0:D, 0:D], start=False, stop=True).then_inc(g_pe, 1)
                    pe.wait_ge(g_dve, i * 9 + 8)
                    pe.matmul(psSums[0][0:GP, 0:ACC], g_same[0:GP, 0:GP], g_msg[0:GP, :], start=True, stop=True).then_inc(g_pe, 1)

        @block_.scalar
        def _(act):
            act.dma_start(b1c[0:D, :], b1.rearrange("(p a) -> p a", a=1)).then_inc(weights_in, 16)
            act.dma_start(b1c[D:P, :], b1.rearrange("(p a) -> p a", a=1)).then_inc(weights_in, 16)
            act.dma_start(coef_b[:, :], coef.rearrange("f a -> a f").to_broadcast([P, D])).then_inc(weights_in, 16)
            act.dma_start(b2f[:, :].rearrange("p (j f) -> p j f", f=D),
                          b2.rearrange("(a c f) -> a c f", a=1, c=1).to_broadcast([3, J, D])).then_inc(weights_in, 16)
            act.wait_ge(src_in, 48)
            nc.scalar.copy(src4f[:, :, :], src4[:, :, :]).then_inc(src_float, 1)
            act.wait_ge(dst_in, 64)
            nc.scalar.copy(dst4f[:, :, :], dst4[:, :, :]).then_inc(dst_float, 1)
            act.wait_ge(consts, 2)
            for W, tile in ((W1, W1d), (W2, W2d)):
                act.dma_start(tile[0:D, 0:D], W).then_inc(matrices_in, 16)
                act.dma_start(tile[D:P, D:P], W).then_inc(matrices_in, 16)
            for t in range(GT):
                n = min(P, T // J - t * P)
                act.wait_ge(src_turned, t + 1)
                nc.scalar.copy(srcT[:, t * P * J:t * P * J + n * J].rearrange("p (g j) -> p j g", j=J),
                               bank[t][:, :].rearrange("p (j g) -> p j g", j=J)[:, :, 0:n]).then_inc(src_back, 1)

            def split_high(n):
                if n < FIRST:
                    return
                q = n % XSLOTS
                act.wait_ge(x_in[q], 16 * (n // XSLOTS + 1))
                late(act, x_stored[q], 16 * (n // XSLOTS))
                nc.scalar.copy(xparts[0:XP, q, :, 0, :], xf[:, q, :, :]).then_inc(x_high, 1)

            split_high(0)
            split_high(1)
            for n in range(XC):
                if n + 2 < XC:
                    split_high(n + 2)
                act.wait_ge(x_rest, n + 1)
                nc.scalar.copy(xparts[0:XP, n % XSLOTS, :, 1, :], xf[:, n % XSLOTS, :, :]).then_inc(x_middle, 1)
                if n == 1:
                    act.wait_ge(dst_rel, 1)
                    for t in range(GT):
                        m = nc.scalar.activation(rel[:, t, :], dst4f[:, t, :], ACT.Identity, bias=minus_base[:, t:t + 1])
                    m.then_inc(rel_ready, 1)
                    act.wait_ge(rel_ready, 1)
                    act.dma_start(rel_dram.rearrange("(t p) e -> p t e", p=P), rel[:, :, :]).then_inc(rel_out, 16)
                    with nc.allow_non_contiguous_dma(reason="512 numbers"):
                        act.dma_start(base_dram.rearrange("a (t p) -> p (a t)", p=P), base_i[:, :]).then_inc(rel_out, 16)
                if n == 3:
                    nc.scalar.activation(dst4f[:, :, :], rel[:, :, :], ACT.Relu, bias=minus_last[:, 0:1], accum_out=viol[:, DST_COLUMN:DST_COLUMN + 1])
                if n == 5:
                    nc.scalar.activation(src4f[:, :, :], rel[:, :, :], ACT.Relu, scale=-1.0, accum_out=viol[:, DST_COLUMN + 1:DST_COLUMN + 2]).then_inc(windows_checked, 1)
                if n in (6, 10, 14):
                    clear_first(act, NB - (CLEARS[0] - (n - 6) // 4) * 14, 14)
            act.wait_ge(flag_ready, 1)
            general = act.value_load(flag_i[0:1, 0:1], min_val=0, max_val=1)

            def step(s, u, i, middle):
                h = u % 2
                if real(s):
                    act.wait_ge(edT_made, s + 1)
                    late(act, h1_made, s - 1)
                    nc.scalar.copy(edT[:, h, :], psT[:, 0:2 * P]).then_inc(edT_ready, 1)
                if real(s - 1):
                    act.wait_ge(x_made, s)
                    late(act, msg_ready, s - 2)
                    nc.scalar.copy(xg[:, 1 - h, :, :], psX[:, 0:J * D]).then_inc(x_ready, 1)
                if real(s - 2):
                    v = (u + 2) % UNROLL
                    act.wait_ge(score_ready, s - 1)
                    nc.scalar.copy(rows[:, v, :, LOW], low_f[:, bass.ds((s - 2) * J, J)])
                    nc.scalar.activation(rows[:, v, :, ATT], score[:, h, :], ACT.Exp).then_inc(att_ready, 1)
                if real(s):
                    act.wait_ge(h1_made, s + 1)
                    late(act, h2_made, s - 1)
                    nc.scalar.activation(h1[:, h, :], psH1[:, 0:2 * P], ACT.Tanh, bias=b1c[:, 0:1]).then_inc(h1_ready, 1)
                if real(s - 2):
                    act.wait_ge(att_ready, s - 1)
                    for j in range(J):
                        m = nc.scalar.mul(rows[:, v, j, 0:D], rows[:, v, j, 0:D], rows[:, v, j, ATT:ATT + 1])
                    m.then_inc(rows_ready, 1)

            def tail(half, r):
                n = half * 2 + r
                act.wait_ge(sum_made, half * (2 * FB) + (TAIL + r * FB + FB))
                late(act, turned_back, n - 1)
                nc.scalar.copy(sumT[r][:, 0:4 * P], psTail[r][0][0:ACC, 0:4 * P])
                nc.scalar.copy(sumT[r][:, 4 * P:FB * P], psTail[r][1][0:ACC, 0:(FB - 4) * P]).then_inc(turned_kept, 1)
                if not (isinstance(n, int) and n < 2):
                    finish(half - 1, r)

            def finish(half, q):
                n = half * 2 + q
                act.wait_ge(y_centred, n + 1)
                for k in range(FB):
                    m = nc.scalar.activation(sq[:, q, k, :], y[:, q, k, :], ACT.Square, accum_out=var[:, q, k, :])
                m.then_inc(y_squared, 1)
                act.wait_ge(y_squared, n + 1)
                nc.scalar.activation(var[:, q, :, :], var[:, q, :, :], ACT.Sqrt, scale=1.0 / D, bias=eps[:, 0:1]).then_inc(std_ready, 1)
                act.wait_ge(rstd_ready, n + 1)
                for k in range(FB):
                    m = nc.scalar.mul(y[:, q, k, :], y[:, q, k, :], var[:, q, k, :])
                m.then_inc(y_ready, 1)
                act.wait_ge(y_ready, n + 1)
                b = n * FB
                if not isinstance(n, int) or n < NF - 1:
                    act.dma_start(out[bass.ds(b * P, FB * P), :].rearrange("(b p) f -> p b f", p=P), y[:, q, :, :]).then_inc(out_done[q], 16)
                else:
                    act.dma_start(out[b * P:(b + FB - 1) * P, :].rearrange("(b p) f -> p b f", p=P), y[:, q, 0:FB - 1, :]).then_inc(out_done[q], 16)
                    act.dma_start(out[(NB - 1) * P:N, :], y[0:NL, q, FB - 1, :]).then_inc(out_done[q], 16)

            with act.If(general < 1):
                act.wait_ge(low_ready, 1)
                act.wait_ge(weights_in, 16 * 4)
                run_steps(act, step, lambda *a: None, lambda g, b, k: None)
                for half in range(2):
                    tail(half, 0)
                    tail(half, 1)
                with act.Fori(2, NF // 2) as half:
                    tail(half, 0)
                    tail(half, 1)
                finish(NF // 2 - 1, 0)
                finish(NF // 2 - 1, 1)
            with act.Else():
                act.wait_ge(weights_in, 16 * 4)
                with act.Fori(0, GN) as i:
                    act.wait_ge(g_pe, i * 4 + 1)
                    nc.scalar.copy(g_edT[:, 0:GP], psT[0:D, 0:GP]).then_inc(g_act, 1)
                    act.wait_ge(g_pe, i * 4 + 2)
                    nc.scalar.activation(g_h1[:, 0:GP], psH1[0:D, 0:GP], ACT.Tanh, bias=b1c[0:D, 0:1]).then_inc(g_act, 1)
                    act.wait_ge(g_dve, i * 9 + 7)
                    nc.scalar.activation(g_n[0:GP, 2:3], g_n[0:GP, 1:2], ACT.Exp).then_inc(g_act, 1)
                for n in range(NF):
                    finish(n // 2, n % 2)
            act.wait_ge(out_done[0], 16 * (NF // 2))
            act.wait_ge(out_done[1], 16 * (NF // 2 + 1))

        @block_.vector
        def _(dve):
            at = [0]

            def link(ins):
                at[0] += 1
                ins.then_inc(dve_step, 1)
                dve.wait_ge(dve_step, at[0])

            nc.vector.memset(src4[:, :, :], NB * P).then_inc(memset_done, 1)
            nc.vector.memset(dst4[:, :, :], 0).then_inc(memset_done, 1)
            nc.vector.memset(W1d[:, :], 0.0)
            nc.vector.memset(W2d[:, :], 0.0)
            nc.vector.memset(ones_f[:, :], 1.0)
            nc.vector.memset(minus_last[:, :], -(P - 1.0))
            nc.vector.memset(eps[:, :], 1e-5)
            nc.vector.memset(ones_b[:, :], 1.0)
            dve.wait_ge(iotas, 2 + PARTS)
            nc.vector.tensor_copy(iota_n[:, :], iota_i[:, :])
            link(nc.vector.tensor_copy(part[:, :], part_i[:, :]))
            nc.vector.tensor_scalar(ident[:, :], iota_n[:, :], part[:, 0:1], None, ALU.is_equal).then_inc(consts, 1)
            nc.vector.tensor_copy(iota_b[:, :], iota_n[:, :])
            nc.vector.tensor_scalar(earlier[:, :], iota_n[:, :], part[:, 0:1], None, ALU.is_gt)
            nc.vector.tensor_scalar(later_f[:, :], iota_n[:, :], part[:, 0:1], None, ALU.is_lt)
            nc.vector.tensor_scalar(count_rest[:, :], iota_n[:, :], part[:, 0:1], None, ALU.is_le)
            nc.vector.tensor_scalar(digit_i[:, 0:1], part_i[:, :], 3, None, ALU.logical_shift_right)
            nc.vector.tensor_scalar(digit_i[:, 1:2], part_i[:, :], NHI - 1, None, ALU.bitwise_and)
            for c in range(PARTS):
                nc.vector.tensor_scalar(start_f[0:1, c, :], start_i[0:1, c, :], -BIG, None, ALU.add)
            link(nc.vector.memset(maskt[:, :], 0.0))
            nc.vector.memset(start_f[0:1, 0, NB:NBK], float(DUMP) - BIG)
            nc.vector.memset(start_f[0:1, 1, NB:NBK], float(DUMP) - BIG)
            nc.vector.scalar_tensor_tensor(out=count_own[:, :], in0=ident[:, :], scalar=BIG, in1=earlier[:, :], op0=ALU.mult, op1=ALU.add)
            nc.vector.tensor_scalar(drop_own[:, :], ident[:, :], -BIG, None, ALU.mult)
            link(nc.vector.tensor_copy(digit[:, :], digit_i[:, :]))
            nc.vector.tensor_scalar(maskt[:, :], iota_n[:, 0:NLO], digit[:, 0:1], None, ALU.is_equal)
            nc.vector.tensor_scalar(maskk[:, :], iota_n[:, 0:NHI], digit[:, 1:2], None, ALU.is_equal).then_inc(consts, 1)
            dve.wait_ge(weights_in, 16 * 4)
            link(nc.vector.tensor_copy(b2h[:, :], b2f[:, :]))
            link(nc.vector.tensor_scalar(b2s[:, :], b2h[:, :], ident[0:3, 0:1], None, ALU.mult))
            for k in (1, 2):
                link(nc.vector.tensor_tensor(b2f[:, :], b2f[:, :], b2h[:, :], ALU.subtract))
                link(nc.vector.tensor_copy(b2h[:, :], b2f[:, :]))
                link(nc.vector.tensor_scalar(b2r[:, :], b2h[:, :], ident[0:3, k:k + 1], None, ALU.mult))
                link(nc.vector.tensor_tensor(b2s[:, :], b2s[:, :], b2r[:, :], ALU.add))
            nc.vector.tensor_copy(b2p[:, :], b2s[:, :]).then_inc(b2_ready, 1)
            dve.wait_ge(dst_float, 1)
            link(nc.vector.tensor_scalar(base_f[:, :], dst4f[:, :, 0], float(LAST_WINDOW), None, ALU.min))
            nc.vector.tensor_scalar(minus_base[:, :], base_f[:, :], -1.0, None, ALU.mult)
            nc.vector.tensor_copy(base_i[:, :], base_f[:, :]).then_inc(dst_rel, 1)
            dve.wait_ge(src_back, GT)
            nc.vector.tensor_scalar(loT[:, :], srcT[:, :], 7, NLO - 1, ALU.logical_shift_right, ALU.bitwise_and)
            link(nc.vector.tensor_scalar(hiT[:, :], srcT[:, :], 11, None, ALU.logical_shift_right))
            link(nc.vector.tensor_copy(lo_b[:, :], loT[:, :]))
            for t0, t1 in ((0, STARTS[2] * J), (STARTS[2] * J, T)):
                for k in range(NHI):
                    nc.vector.tensor_scalar(hot_hi[:, t0:t1, k], hiT[:, t0:t1], float(k), None, ALU.is_equal)
                for k in range(NLO):
                    m = nc.vector.tensor_scalar(hot_lo[:, k, t0:t1], lo_b[:, t0:t1], float(k), None, ALU.is_equal)
                m.then_inc(digits, 1)
            dve.wait_ge(digits, 2)
            nc.vector.tensor_scalar(loT[:, :], srcT[:, :], P - 1, None, ALU.bitwise_and)
            link(nc.vector.tensor_scalar(hiT[:, :], srcT[:, :], 7, None, ALU.logical_shift_right))
            nc.vector.tensor_copy(low_f[:, :], loT[:, :])
            nc.vector.tensor_copy(block_b[:, :], hiT[:, :]).then_inc(low_ready, 1)
            dve.wait_ge(low_ready, 1)
            for c in range(0, PARTS, 2):
                dve.wait_ge(hist_made, c // 2 + 1)
                link(nc.vector.tensor_tensor(hist_m[:, c:c + 2, :, :].rearrange("p c l t -> p (c l) t"), bank[6 + c // 2][:, :].rearrange("p (l t) -> p l t", t=NLO),
                                             maskt[:, :].rearrange("p (a t) -> p a t", a=1).to_broadcast([P, 2 * NLO, NLO]), ALU.mult))
                link(nc.vector.tensor_reduce(hist_r[:, c:c + 2, :], hist_m[:, c:c + 2, :, :], AX.X, ALU.add))
                for d in range(c, c + 2):
                    m = nc.vector.tensor_tensor(hist_x[:, d, :, :], hist_r[:, d:d + 1, :].to_broadcast([P, NHI, NLO]),
                                                maskk[:, :].rearrange("p (k a) -> p k a", a=1).to_broadcast([P, NHI, NLO]), ALU.mult)
            m.then_inc(hist_ready, 1)
            dve.wait_ge(counts_made, 1)
            counts = bank[5][:, 0:PARTS * NHI * NLO].rearrange("p (c b) -> p c b", c=PARTS)[:, :, 0:NB]
            nc.vector.tensor_reduce(viol[:, 0:PARTS], counts, AX.X, ALU.max)
            link(nc.vector.tensor_reduce(viol[:, PARTS:2 * PARTS], counts[:, :, 0:NB - 1], AX.X, ALU.min))
            for c in range(PARTS):
                nc.vector.tensor_scalar(viol[:, c:c + 1], viol[:, c:c + 1], float(CAP[c] * P), None, ALU.is_gt)
                m = nc.vector.tensor_scalar(viol[:, PARTS + c:PARTS + c + 1], viol[:, PARTS + c:PARTS + c + 1], float(FULL[c]), None, ALU.is_lt)
            m.then_inc(viol_ready, 1)
            dve.wait_ge(viol_made, 1)
            link(nc.vector.tensor_reduce(viol[:, 0:1], bank[4][:, 0:2 * PARTS + 2], AX.X, ALU.max))
            nc.vector.tensor_scalar(flag_i[0:1, 0:1], viol[0:1, 0:1], 0.0, None, ALU.is_gt).then_inc(flag_ready, 1)
            dve.wait_ge(flag_ready, 1)
            general = dve.value_load(flag_i[0:1, 0:1], min_val=0, max_val=1)
            coef_j = coef_b[:, :].rearrange("p (a f) -> p a f", a=1).to_broadcast([P, J, D])
            iota_j = iota_b[:, 0:NBK].rearrange("p (a b) -> p a b", a=1).to_broadcast([P, J, NBK])

            def make_hot(s, u):
                late(dve, counted, s - 1)
                nc.vector.tensor_tensor(hot[:, u % 2, :, :], iota_j,
                                        block_b[:, bass.ds(s * J, J)].rearrange("p (j a) -> p j a", a=1).to_broadcast([P, J, NBK]),
                                        ALU.is_equal).then_inc(hot_ready, 1)

            def step(s, u, i, middle):
                h = u % 2
                if isinstance(s, int) and s == 0:
                    make_hot(0, 0)
                if real(s):
                    dve.wait_ge(rank_made, s + 1)
                    late(dve, scattered[u], i * (16 * J))
                    nc.vector.tensor_reduce(slot[:, u, :], psRank[:, 0:J * NBK].rearrange("p (j b) -> p j b", j=J), AX.X, ALU.max).then_inc(slot_ready, 1)
                    dve.wait_ge(rel_spread, s + 1)
                    late(dve, x_made, s - 1)
                    nc.vector.tensor_scalar(onehot[:, h, :], psRel[:, :], part[:, 0:1], None, ALU.is_equal).then_inc(onehot_ready, 1)
                middle()
                if real(s - 1):
                    v = (u - 1) % UNROLL
                    dve.wait_ge(h2_made, s)
                    dve.wait_ge(x_ready, s)
                    nc.vector.tensor_tensor(rows[:, v, :, 0:D], psH2[:, 0:J * D].rearrange("p (j f) -> p j f", j=J),
                                            xg[:, 1 - h, :, :], ALU.mult).then_inc(msg_ready, 1)
                if real(s + 1) and not (isinstance(s, int) and s + 1 == NG):
                    make_hot(s + 1, u + 1)
                if real(s - 1):
                    dve.wait_ge(msg_ready, s)
                    late(dve, score_ready, s - 1)
                    nc.vector.tensor_tensor(weighted[:, :, :], rows[:, v, :, 0:D], coef_j, ALU.mult).then_inc(weighted_ready, 1)
                    dve.wait_ge(weighted_ready, s)
                    late(dve, att_ready, s - 2)
                    nc.vector.tensor_reduce(score[:, 1 - h, :], weighted[:, :, :], AX.X, ALU.add).then_inc(score_ready, 1)

            def picks(to, low):
                shape = [P, to.shape[1], P]
                return nc.vector.tensor_tensor(to, iota_n[:, :].rearrange("p (a n) -> p a n", a=1).to_broadcast(shape),
                                               low.to_broadcast(shape), ALU.is_equal)

            def keep(g, b, u):
                if isinstance(g, int) and g == 0:
                    dve.wait_ge(acc_cleared, 1)
                dve.wait_ge(sum_made, g + 1)
                nc.vector.tensor_tensor(acc[:, bass.ds(b, 1), :], acc[:, bass.ds(b, 1), :],
                                        psSums[u % 2][:, 0:ACC].rearrange("p (b f) -> p b f", b=1), ALU.add).then_inc(sum_kept, 1)

            def block(g, b, u, use, prev, c):
                if not (isinstance(b, int) and b <= LAG):
                    keep(g - (LAG + 1), b - (LAG + 1), u + LAG + 1)
                dve.wait_ge(back0_in[u], use * 16 + 16)
                if prev is not None:
                    dve.wait_ge(sum_made, prev + 1)
                picks(pick0[:, u, :, :], back0[:, u, :, LOW:LOW + 1]).then_inc(pick_ready, 1)

            def drain(g, b, k):
                k -= LAG + 1
                keep(g + k, b + k, k)

            def tail(i, r):
                n = i + r
                for k in range(FB):
                    dve.wait_ge(back1_in[k], (n + 1) * 16)
                    if not (isinstance(n, int) and n == 0):
                        dve.wait_ge(sum_made, i * FB + (TAIL + r * FB + k + 1 - FB))
                    picks(pick1[:, k, :, :], back1[:, k, :, LOW:LOW + 1]).then_inc(pick_ready, 1)
                    behind(i, r, k)

            def behind(i, r, k):
                if k == 2:
                    add_sums(i, r - 2)
                if k == 3:
                    finish_third(i, r - 3)
                if k == 5:
                    finish_second(i, r - 2)

            def none_such(i, r):
                return isinstance(i, int) and not 0 <= i + r < NF

            def add_sums(i, r):
                if none_such(i, r):
                    return
                b = i * FB + r * FB
                dve.wait_ge(turned_back, i + (r + 1))
                nc.vector.tensor_tensor(acc[:, bass.ds(b, FB), :], acc[:, bass.ds(b, FB), :],
                                        psSums[r % 2][:, 0:FB * ACC].rearrange("p (b f) -> p b f", b=FB), ALU.add).then_inc(sums_ready, 1)
                finish_first(i, r)

            def finish_first(i, r):
                n, q = i + r, r % 2
                b = n * FB
                dve.wait_ge(sums_ready, n + 1)
                late(dve, y_scaled, n - 1)
                nc.vector.tensor_scalar(fix[:, q, :, :], acc[:, bass.ds(b, FB), D:D + 1], 0.0, None, ALU.is_le).then_inc(fixed, 1)
                dve.wait_ge(fixed, n + 1)
                nc.vector.tensor_tensor(fix[:, q, :, :], acc[:, bass.ds(b, FB), D:D + 1], fix[:, q, :, :], ALU.add).then_inc(den_added, 1)
                dve.wait_ge(den_added, n + 1)
                nc.vector.reciprocal(den[:, q, :, :], fix[:, q, :, :]).then_inc(den_ready, 1)

            def finish_second(i, r):
                if none_such(i, r):
                    return
                n, q = i + r, r % 2
                dve.wait_ge(y_added, n + 1)
                nc.vector.tensor_reduce(mean[:, q, :, 0], y[:, q, :, :], AX.X, ALU.add).then_inc(y_summed, 1)
                dve.wait_ge(y_summed, n + 1)
                nc.vector.tensor_scalar(mean[:, q, :, :], mean[:, q, :, :], 1.0 / D, None, ALU.mult).then_inc(mean_ready, 1)

            def finish_third(i, r):
                if none_such(i, r):
                    return
                n, q = i + r, r % 2
                dve.wait_ge(std_ready, n + 1)
                nc.vector.reciprocal(var[:, q, :, :], var[:, q, :, :]).then_inc(rstd_ready, 1)

            with dve.If(general < 1):
                run_steps(dve, step, block, drain)
                dve.wait_ge(sum_kept, TAIL)
                for n in range(4):
                    tail(n - n % 2, n % 2)
                with dve.Fori(2, NF // 2) as i:
                    tail(i * 2, 0)
                    tail(i * 2, 1)
                for r in range(3):
                    for k in range(FB):
                        behind(NF, r, k)
            with dve.Else():
                with dve.Fori(0, GN) as i:
                    dve.wait_ge(g_in, i * 48 + 48)
                    nc.vector.tensor_copy(g_srcf[0:GP, :], g_src[0:GP, :]).then_inc(g_dve, 1)
                    dve.wait_ge(g_dve, i * 9 + 1)
                    nc.vector.tensor_scalar(g_srcb[0:GP, :], iota_n[0:GP, :], 0.0, g_srcf[0:GP, 0:1], ALU.mult, ALU.add).then_inc(g_dve, 1)
                    dve.wait_ge(g_pe, i * 4 + 1)
                    nc.vector.tensor_scalar(g_same[0:GP, 0:GP], psRel[0:GP, 0:GP], g_srcf[0:GP, 0:1], None, ALU.is_equal).then_inc(g_dve, 1)
                    dve.wait_ge(g_dve, i * 9 + 3)
                    nc.vector.tensor_tensor(g_prev[0:GP, 0:GP], g_same[0:GP, 0:GP], later_f[0:GP, 0:GP], ALU.mult).then_inc(g_dve, 1)
                    dve.wait_ge(g_pe, i * 4 + 3)
                    dve.wait_ge(g_gathered, i * 32 + 32)
                    nc.vector.tensor_tensor(g_msg[0:GP, 0:D], psH2[0:GP, 0:D], g_x[0:GP, :], ALU.mult).then_inc(g_dve, 1)
                    dve.wait_ge(g_dve, i * 9 + 5)
                    nc.vector.tensor_tensor(g_t[0:GP, :], g_msg[0:GP, 0:D], coef_b[0:GP, :], ALU.mult).then_inc(g_dve, 1)
                    dve.wait_ge(g_dve, i * 9 + 6)
                    nc.vector.tensor_reduce(g_n[0:GP, 1:2], g_t[0:GP, :], AX.X, ALU.add).then_inc(g_dve, 1)
                    nc.vector.tensor_reduce(g_n[0:GP, 0:1], g_prev[0:GP, 0:GP], AX.X, ALU.max)
                    dve.wait_ge(g_act, i * 3 + 3)
                    nc.vector.tensor_copy(g_msg[0:GP, D:D + 1], g_n[0:GP, 2:3])
                    nc.vector.tensor_scalar(g_msg[0:GP, 0:D], g_msg[0:GP, 0:D], g_n[0:GP, 2:3], None, ALU.mult).then_inc(g_dve, 1)
                    dve.wait_ge(g_dve, i * 9 + 8)
                    nc.vector.scalar_tensor_tensor(out=g_n[0:GP, 3:4], in0=part[0:GP, :], scalar=float(NB * P), in1=g_srcf[0:GP, :], op0=ALU.add, op1=ALU.subtract)
                    dve.wait_ge(g_pe, i * 4 + 4)
                    nc.vector.tensor_tensor(g_msg[0:GP, :], psSums[0][0:GP, 0:ACC], g_sum[0:GP, :], ALU.add)
                    dve.drain()
                    nc.vector.scalar_tensor_tensor(out=g_to[0:GP, :], in0=g_n[0:GP, 3:4], scalar=g_n[0:GP, 0:1], in1=g_srcf[0:GP, :], op0=ALU.mult, op1=ALU.add).then_inc(g_dve, 1)
                dve.wait_ge(g_done, GN * 16)
                dve.wait_ge(g_back, 16)
                nc.vector.engine_nop().then_inc(sums_ready, NF)
                for i in range(0, NF, 2):
                    for r in range(2):
                        finish_first(i, r)
                        finish_second(i, r)
                        finish_third(i, r)


_INS = ["x", "src", "dst", "edge_attr_64", "L0_gnn_W1", "L0_gnn_b1", "L0_gnn_W2", "L0_gnn_b2", "L0_gnn_linear_coef"]


def kernel(**inputs):
    import numpy as _np
    import concourse.bacc as _bacc
    from concourse import mybir as _mybir
    from concourse.bass_utils import run_bass_kernel_spmd as _run

    nc = _bacc.Bacc("TRN2", target_bir_lowering=False, num_devices=1)
    arrays, args = {}, []
    for name in _INS:
        a = _np.ascontiguousarray(inputs[name])
        arrays[f"in_{name}"] = a
        args.append(nc.dram_tensor(f"in_{name}", a.shape, _mybir.dt.from_np(a.dtype), kind="ExternalInput").ap())
    shape = inputs["x"].shape
    args.append(nc.dram_tensor("out", shape, _mybir.dt.float32, kind="ExternalOutput").ap())
    node_sums_kernel(nc, *args)
    r = _run(nc, [arrays], core_ids=[0])
    return r.results[0]["out"]
```
